# Optimizing a Trainium2 kernel written in Bass

```python
import numpy as np
import jax
import jax.numpy as jnp

def _softmax(x, axis=-1):
    return jax.nn.softmax(x, axis=axis)

def _gelu(x):
    return jax.nn.gelu(x, approximate=True)

def _silu(x):
    return jax.nn.silu(x)

def _sigmoid(x):
    return jax.nn.sigmoid(x)

def _layernorm(x, axis=-1, eps=1e-05):
    m = jnp.mean(x, axis=axis, keepdims=True)
    v = jnp.var(x, axis=axis, keepdims=True)
    return (x - m) / jnp.sqrt(v + eps)

def _scatter_add(tgt, idx, src, axis=0):
    return tgt.at[idx].add(src)

def _segment_sum(src, seg, n):
    return jax.ops.segment_sum(src, seg, n)
kernel_name = 'mk_gnn_preln_d1_gnn_r8_a7d820'

def setup_inputs(seed: int=0):
    np.random.seed(seed)
    _w = jnp.asarray

    def _rec_inputs():
        import jax
        import jax.numpy as jnp
        _gk = jax.random.key(seed)
        x = 1.875e-06 + 0.1 * jax.random.normal(jax.random.fold_in(_gk, 1), (18750, 64), jnp.float32)
        _s = jax.random.randint(jax.random.fold_in(_gk, 2), (150000,), 0, 18750, jnp.int32)
        _d = jax.random.randint(jax.random.fold_in(_gk, 3), (150000,), 0, 18750, jnp.int32)
        _loop = jnp.arange(18750, dtype=jnp.int32)
        src = jnp.concatenate([_s, _d, _loop])
        dst = jnp.concatenate([_d, _s, _loop])
        _o = jnp.argsort(dst, stable=True)
        src = src[_o]
        dst = dst[_o]
        edge_weight1 = jax.random.uniform(jax.random.fold_in(_gk, 12), (318750, 1), jnp.float32, 0.0, 0.999998)
        return (x, src, dst, edge_weight1)
    x, src, dst, edge_weight1 = _rec_inputs()

    def _L0_gnn_setup():
        import jax, jax.numpy as jnp
        import numpy as np
        GAMMA = -0.45
        ZETA = 1.05
        EPS_NOISE = 1e-07
        EPS_DEG = 1e-06
        N_NODES = 18750
        N_EDGES = 125000
        DIM = 64

        def _denoise_gcn_layer(x, row, col, noise, nbW, nbb, selfW, selfb, attW, attb):
            f1 = x[row]
            f2 = x[col]
            h1 = jax.nn.relu(f1 @ nbW + nbb)
            h2 = jax.nn.relu(f2 @ selfW + selfb)
            log_alpha = jnp.concatenate([h1, h2], axis=1) @ attW + attb
            u = jnp.clip(noise, EPS_NOISE, 1.0 - EPS_NOISE)
            gate = jax.nn.sigmoid(jnp.log(u) - jnp.log1p(-u) + log_alpha)
            mask = jnp.clip(gate * (ZETA - GAMMA) + GAMMA, 0.0, 1.0)[:, 0]
            rowsum = jax.ops.segment_sum(mask, row, num_segments=N_NODES) + EPS_DEG
            d_inv_sqrt = jnp.clip(rowsum ** (-0.5), 0.0, 10.0)
            vals = mask * d_inv_sqrt[row] * d_inv_sqrt[col]
            msg = vals[:, None] * f2
            return jax.ops.segment_sum(msg, row, num_segments=N_NODES)
        key = jax.random.key(seed)
        ks = jax.random.split(key, 16)
        features = jax.random.normal(ks[0], (N_NODES, DIM), dtype=jnp.float32) * 0.1
        row = jax.random.randint(ks[1], (N_EDGES,), 0, N_NODES, dtype=jnp.int32)
        col = jax.random.randint(ks[2], (N_EDGES,), 0, N_NODES, dtype=jnp.int32)
        noise0 = jax.random.uniform(ks[3], (N_EDGES, 1), dtype=jnp.float32)
        noise1 = jax.random.uniform(ks[4], (N_EDGES, 1), dtype=jnp.float32)
        s = 1.0 / np.sqrt(DIM)

        def lin(k, fan_in, fan_out):
            return jax.random.uniform(k, (fan_in, fan_out), jnp.float32, -s, s)
        params = {'nbW0': lin(ks[5], DIM, DIM), 'nbb0': jnp.zeros((DIM,), jnp.float32), 'selfW0': lin(ks[6], DIM, DIM), 'selfb0': jnp.zeros((DIM,), jnp.float32), 'attW0': lin(ks[7], 2 * DIM, 1), 'attb0': jnp.zeros((1,), jnp.float32), 'nbW1': lin(ks[8], DIM, DIM), 'nbb1': jnp.zeros((DIM,), jnp.float32), 'selfW1': lin(ks[9], DIM, DIM), 'selfb1': jnp.zeros((DIM,), jnp.float32), 'attW1': lin(ks[10], 2 * DIM, 1), 'attb1': jnp.zeros((1,), jnp.float32)}
        return dict(features=features, row=row, col=col, noise0=noise0, noise1=noise1, **params)
    _L0_gnn_all = _L0_gnn_setup()
    _L0_gnn_in = {k: v for k, v in _L0_gnn_all.items() if k in ('nbW0', 'nbb0', 'selfW0', 'selfb0', 'attW0', 'attb0', 'nbW1', 'nbb1', 'selfW1', 'selfb1', 'attW1', 'attb1')}
    del _L0_gnn_all
    return {'x': x, 'src': src, 'dst': dst, 'edge_weight1': edge_weight1, 'L0_gnn_nbW0': _L0_gnn_in['nbW0'], 'L0_gnn_nbb0': _L0_gnn_in['nbb0'], 'L0_gnn_selfW0': _L0_gnn_in['selfW0'], 'L0_gnn_selfb0': _L0_gnn_in['selfb0'], 'L0_gnn_attW0': _L0_gnn_in['attW0'], 'L0_gnn_attb0': _L0_gnn_in['attb0'], 'L0_gnn_nbW1': _L0_gnn_in['nbW1'], 'L0_gnn_nbb1': _L0_gnn_in['nbb1'], 'L0_gnn_selfW1': _L0_gnn_in['selfW1'], 'L0_gnn_selfb1': _L0_gnn_in['selfb1'], 'L0_gnn_attW1': _L0_gnn_in['attW1'], 'L0_gnn_attb1': _L0_gnn_in['attb1']}

def reference(x, src, dst, edge_weight1, L0_gnn_nbW0, L0_gnn_nbb0, L0_gnn_selfW0, L0_gnn_selfb0, L0_gnn_attW0, L0_gnn_attb0, L0_gnn_nbW1, L0_gnn_nbb1, L0_gnn_selfW1, L0_gnn_selfb1, L0_gnn_attW1, L0_gnn_attb1):
    import jax
    import jax.numpy as jnp

    def _L0_gnn_ref(features, row, col, noise0, noise1, nbW0, nbb0, selfW0, selfb0, attW0, attb0, nbW1, nbb1, selfW1, selfb1, attW1, attb1):
        import jax, jax.numpy as jnp
        import numpy as np
        GAMMA = -0.45
        ZETA = 1.05
        EPS_NOISE = 1e-07
        EPS_DEG = 1e-06
        N_NODES = 18750
        N_EDGES = 125000
        DIM = 64

        def _denoise_gcn_layer(x, row, col, noise, nbW, nbb, selfW, selfb, attW, attb):
            f1 = x[row]
            f2 = x[col]
            h1 = jax.nn.relu(f1 @ nbW + nbb)
            h2 = jax.nn.relu(f2 @ selfW + selfb)
            log_alpha = jnp.concatenate([h1, h2], axis=1) @ attW + attb
            u = jnp.clip(noise, EPS_NOISE, 1.0 - EPS_NOISE)
            gate = jax.nn.sigmoid(jnp.log(u) - jnp.log1p(-u) + log_alpha)
            mask = jnp.clip(gate * (ZETA - GAMMA) + GAMMA, 0.0, 1.0)[:, 0]
            rowsum = jax.ops.segment_sum(mask, row, num_segments=N_NODES) + EPS_DEG
            d_inv_sqrt = jnp.clip(rowsum ** (-0.5), 0.0, 10.0)
            vals = mask * d_inv_sqrt[row] * d_inv_sqrt[col]
            msg = vals[:, None] * f2
            return jax.ops.segment_sum(msg, row, num_segments=N_NODES)
        x0 = features
        x1 = _denoise_gcn_layer(x0, row, col, noise0, nbW0, nbb0, selfW0, selfb0, attW0, attb0)
        x2 = _denoise_gcn_layer(x1, row, col, noise1, nbW1, nbb1, selfW1, selfb1, attW1, attb1)
        return x0 + x1 + x2
    h = jnp.maximum(_layernorm(x, axis=-1), 0.0)
    x = x + _L0_gnn_ref(h, src, dst, edge_weight1, edge_weight1, L0_gnn_nbW0, L0_gnn_nbb0, L0_gnn_selfW0, L0_gnn_selfb0, L0_gnn_attW0, L0_gnn_attb0, L0_gnn_nbW1, L0_gnn_nbb1, L0_gnn_selfW1, L0_gnn_selfb1, L0_gnn_attW1, L0_gnn_attb1)
    return x

_drawn_inputs = setup_inputs


def setup_inputs(seed=0):
    import zlib

    import numpy as np

    out = dict(_drawn_inputs(seed))
    spreads = {'L0_gnn_nbb0': (0.0, 0.8),
     'L0_gnn_selfb0': (0.0, 0.8),
     'L0_gnn_nbb1': (0.0, 0.8),
     'L0_gnn_selfb1': (0.0, 0.8)}
    factors = {'L0_gnn_nbW0': 3.231,
     'L0_gnn_selfW0': 2.739,
     'L0_gnn_nbW1': 8.0,
     'L0_gnn_selfW1': 8.0,
     'L0_gnn_attW1': 8.0}
    for name, (base, spread) in spreads.items():
        noise = np.random.default_rng([zlib.crc32(name.encode()), seed]).standard_normal(out[name].shape)
        drawn = base * np.exp(spread * noise) if base else spread * noise
        out[name] = jnp.asarray(drawn.astype(out[name].dtype))
    for name, factor in factors.items():
        out[name] = (out[name] * factor).astype(out[name].dtype)
    return out
```

```python
import concourse.bass as bass
from concourse import mybir
from contextlib import ExitStack

N, D, E = 18750, 64, 318750
P = 128
HI = -(-N // P)
NP = P * HI
CH = 8
SE = CH * P
RJ = 3
RP = -(-E // (SE * RJ))
NS = RP * RJ
NC = NS * CH
RW = RJ * SE
EP = NS * SE
PAD_ROW = NP
TABLE_ROWS = NP + P
GAMMA, ZETA = -0.45, 1.05
EPS_NOISE, EPS_DEG, EPS_LN = 1e-7, 1e-6, 1e-5
PIECES = 7
PH = HI // PIECES
PW = PH * D
ZW = TABLE_ROWS * D // P // 8
GH = 3
NG = HI // GH
assert HI % PIECES == 0 and HI % GH == 0 and NG % 2 == 1 and NS % 2 == 0


def build(nc, x, src, dst, noise, params, out):
    f32, bf16, i32, u16 = mybir.dt.float32, mybir.dt.bfloat16, mybir.dt.int32, mybir.dt.uint16
    ALU, ACT, AX = mybir.AluOpType, mybir.ActivationFunctionType, mybir.AxisListType

    row_d = nc.dram_tensor("row_d", (EP,), u16).ap()
    rlo_d = nc.dram_tensor("rlo_d", (EP,), u16).ap()
    clo_d = nc.dram_tensor("clo_d", (EP,), u16).ap()
    acc_d = nc.dram_tensor("acc_d", (P, HI * D), f32).ap()
    y_d = [nc.dram_tensor(f"y_d{L}", (NP, D), f32).ap() for L in range(2)]
    tab_d = [[nc.dram_tensor(f"tab_d{L}_{k}", (TABLE_ROWS, D), f32).ap() for k in range(CH)] for L in range(2)]

    ctx = ExitStack()
    with ctx:
        def sb(name, shape, dt):
            return ctx.enter_context(nc.sbuf_tensor(name, shape, dt))

        def sem(name):
            return ctx.enter_context(nc.semaphore(name))

        cur = sb("cur", [P, HI * D], f32)
        work = sb("work", [P, HI * D], f32)
        rowf = sb("rowf", [P, NC], f32)
        lof = sb("lof", [P, NC], f32)
        hif = sb("hif", [P, NC], f32)
        chif = sb("chif", [P, NC], f32)
        coli = sb("coli", [P, NC], i32)
        logit = sb("logit", [P, NC], f32)
        ga = sb("ga", [P, NC], f32)
        gb = sb("gb", [P, NC], f32)
        ones_lo = sb("ones_lo", [P, 2, SE], bf16)
        lo_bc = sb("lo_bc", [P, 2, SE], u16)
        row_bc = sb("row_bc", [P, 2, SE], u16)
        Z = sb("Z", [P, CH * (P + HI)], f32)
        G = sb("G", [P, 2, CH, D], f32)
        Sw = sb("Sw", [P, 2, CH, P], f32)
        Mo = sb("Mo", [P, 2, CH, D], f32)
        zero = sb("zero", [P, ZW], f32)
        iota = sb("iota", [P, HI], f32)
        pid = sb("pid", [P, 1], f32)
        trash = sb("trash", [P, 1], f32)
        ident = sb("ident", [P, P], f32)
        earlier = sb("earlier", [P, P], f32)
        W = [sb(f"W{L}", [D, 2 * D], f32) for L in range(2)]
        bias = [sb(f"bias{L}", [P, 1], f32) for L in range(2)]
        att = [sb(f"att{L}", [P, 2], f32) for L in range(2)]
        attb = [sb(f"attb{L}", [P, 1], f32) for L in range(2)]
        ab = sb("ab", [P, HI, 2], f32)
        abs3 = sb("abs3", [P, 3, 2, HI], bf16)
        abr = sb("abr", [P, 2, HI], f32)
        st = sb("st", [P, 2, PH], f32)
        eps = sb("eps", [P, 2], f32)
        dinv = sb("dinv", [P, HI], f32)
        ridx = sb("ridx", [P, 2, CH], i32)
        cidx = sb("cidx", [P, 2, CH], i32)
        cnt = sb("cnt", [P, CH], f32)
        dtmp = sb("dtmp", [P, CH], f32)
        psG = ctx.enter_context(nc.psum_tensor("psG", [P, 6, 512], f32))
        psR = ctx.enter_context(nc.psum_tensor("psR", [P, 512], f32))
        OA = Z[:, 0:CH * P].rearrange("p (k n) -> p k n", k=CH)
        OB = Z[:, CH * P:CH * (P + HI)].rearrange("p (k n) -> p k n", k=CH)
        junk = [t.rearrange("p (k n) -> p k n", k=CH) for t in
                (Sw[:, :, :, :].rearrange("p a k n -> p (a k n)")[:, 0:CH * HI], Z[:, 0:CH * HI])]
        junk2 = sb("junk2", [P, CH, P], f32)
        Xs = Z[:, 1536:1536 + 2 * GH * D].rearrange("p (s n) -> p s n", s=2)
        X = [work, cur]
        Y = [cur, work]
        A = [work[0:RP, i * RW:(i + 1) * RW] for i in range(3)]
        B = [cur[0:RP, i * RW:(i + 1) * RW] for i in range(3)]
        U = [t[0:RP, 0:RW // 2].bitcast(u16) for t in (logit, ga, gb)]

        s_pad, s_const, s_w, s_x = sem("s_pad"), sem("s_const"), sem("s_w"), sem("s_x")
        s_row, s_col, s_nz = sem("s_row"), sem("s_col"), sem("s_nz")
        s_u16, s_scr = sem("s_u16"), sem("s_scr")
        s_split, s_tp, s_tpe = sem("s_split"), sem("s_tp"), sem("s_tpe")
        s_dve, s_v2a, s_a2v = sem("s_dve"), sem("s_v2a"), sem("s_a2v")
        s_acc, s_accd = sem("s_acc"), sem("s_accd")
        s_stg = sem("s_stg")
        s_T, s_hT, s_mm, s_rT, s_sm, s_ab = (sem(n) for n in ("s_T", "s_hT", "s_mm", "s_rT", "s_sm", "s_ab"))
        s_abs = sem("s_abs")
        s_lo = [sem("s_lo_r"), sem("s_lo_c")]
        s_oh = [sem("s_oh_r"), sem("s_oh_c")]
        s_g = [sem("s_g_r"), sem("s_g_c")]
        s_sel = [sem("s_sel_r"), sem("s_sel_c")]
        s_oab, s_acm, s_R = sem("s_oab"), sem("s_acm"), sem("s_R")
        s_y, s_yd = sem("s_y"), sem("s_yd")
        s_zero = [sem("s_zero0"), sem("s_zero1")]
        s_rb = [sem("s_rb0"), sem("s_rb1")]
        s_cnt, s_idx, s_sw, s_pm, s_mo = (sem(n) for n in ("s_cnt", "s_idx", "s_sw", "s_pm", "s_mo"))
        s_gat = [sem("s_gat0"), sem("s_gat1")]
        s_tab = [sem(f"s_tab{k}") for k in range(CH)]
        s_tl = [sem("s_tl0"), sem("s_tl1")]
        s_add, s_piece, s_outd = sem("s_add"), sem("s_piece"), [sem("s_outd0"), sem("s_outd1")]

        def wait(eng, semaphore, value):
            if not isinstance(value, int) or value > 0:
                eng.wait_ge(semaphore, value)

        def steps(eng, n, body):
            body(0)
            with eng.Fori(1, n - 1) as i:
                body(i)
            body(n - 1)

        def rows_dma(eng, dram, tile, width, total, semaphore):
            full = total // width
            cut = full // 16 * 16
            for a, b in ((0, cut), (cut, full)):
                eng.dma_start(tile[a:b, 0:width], dram[a * width:b * width].rearrange("(p f) -> p f", f=width)).then_inc(semaphore, 16)
            rest = total - full * width
            eng.dma_start(tile[full:full + 1, 0:rest], dram[full * width:total].rearrange("(p f) -> p f", p=1)).then_inc(semaphore, 16)

        def stored(i):
            tail = (N - N // HI * HI) * D
            return 16 * sum(2 + (j * PW < tail) for j in range(i % 2, i + 1, 2))

        xv = x.rearrange("n d -> (n d)")
        block = ctx.enter_context(nc.Block())

        @block.sync
        def _(sp):
            sp.wait_ge(s_pad, 1)
            rows_dma(sp, src, A[0].bitcast(i32), RW, E, s_row)
            sp.wait_ge(s_pad, 2)
            rows_dma(sp, dst, A[1].bitcast(i32), RW, E, s_col)
            sp.wait_ge(s_pad, 3)
            rows_dma(sp, noise.rearrange("e o -> (e o)"), A[2], RW, E, s_nz)
            for L, (nbW, nbb, selfW, selfb, attW, attbias) in enumerate(params):
                sp.dma_start(W[L][:, 0:D], nbW).then_inc(s_w, 16)
                sp.dma_start(W[L][:, D:2 * D], selfW).then_inc(s_w, 16)
                sp.dma_start(bias[L][0:D, :], nbb.rearrange("(d o) -> d o", o=1)).then_inc(s_w, 16)
                sp.dma_start(bias[L][D:P, :], selfb.rearrange("(d o) -> d o", o=1)).then_inc(s_w, 16)
                sp.wait_ge(s_pad, 4)
                sp.dma_start(att[L][0:D, 0:1], attW[0:D, :]).then_inc(s_w, 16)
                sp.dma_start(att[L][D:P, 1:2], attW[D:2 * D, :]).then_inc(s_w, 16)
                sp.dma_start(attb[L][:, :], attbias.rearrange("(a o) -> a o", o=1).to_broadcast([P, 1])).then_inc(s_w, 16)
            for n, d in enumerate((row_d, rlo_d, clo_d)):
                sp.wait_ge(s_u16, n + 1)
                sp.dma_start(d.rearrange("(p f) -> p f", p=RP), U[n]).then_inc(s_scr, 16)
            sp.wait_ge(s_split, 4)
            rows_dma(sp, xv, cur, HI * D, N * D, s_x)
            sp.wait_ge(s_acc, 1)
            sp.dma_start(acc_d, cur[:, :]).then_inc(s_accd, 16)
            sp.wait_ge(s_scr, 48)
            for L in range(2):
                base = L * NS

                def load_lo(i):
                    for t, d in enumerate((rlo_d, clo_d)):
                        wait(sp, s_oh[t], base + i)
                        sp.dma_start(lo_bc[:, t, :], d[bass.ds(i * SE, SE)].rearrange("(o f) -> o f", o=1).to_broadcast([P, SE])).then_inc(s_lo[t], 16)
                steps(sp, NS, load_lo)
                sp.wait_ge(s_y, L + 1)
                sp.dma_start(y_d[L].rearrange("(p f) d -> p (f d)", p=P), Y[L][:, :]).then_inc(s_yd, 16)

                def load_row(i):
                    for h in range(2):
                        wait(sp, s_sw, base + i * 2 + h - 1)
                        sp.dma_start(row_bc[:, h, :], row_d[bass.ds((i * 2 + h) * SE, SE)].rearrange("(o f) -> o f", o=1).to_broadcast([P, SE])).then_inc(s_rb[h], 16)
                steps(sp, NS // 2, load_row)
                for k in range(CH):
                    sp.wait_ge(s_tab[k], 16 * NS * (L + 1))
                sp.wait_ge(s_yd, 16 * (L + 1))
                srcs = [tab_d[L][k][0:NP, :].rearrange("(p f) d -> p (f d)", p=P) for k in range(CH)] + [acc_d] * L
                before = 0 if L == 0 else PIECES * CH
                for i in range(PIECES):
                    for k, s_ in enumerate(srcs):
                        n = before + i * len(srcs) + k
                        if n >= before + 2:
                            sp.wait_ge(s_add, n - 1)
                        sp.dma_start(work[:, (n % 2) * PW:(n % 2 + 1) * PW], s_[:, i * PW:(i + 1) * PW]).then_inc(s_tl[n % 2], 16)
                    if L == 1:
                        sp.wait_ge(s_piece, i + 1)
                        o = work[:, (2 + i % 2) * PW:(3 + i % 2) * PW]
                        a, b = i * PW, (i + 1) * PW
                        full = N // HI
                        tail = (N - full * HI) * D
                        ov = out.rearrange("n d -> (n d)")
                        main = ov[0:full * HI * D].rearrange("(p f) -> p f", f=HI * D)
                        cut = full // 16 * 16
                        sp.dma_start(main[0:cut, a:b], o[0:cut, :]).then_inc(s_outd[i % 2], 16)
                        sp.dma_start(main[cut:full, a:b], o[cut:full, :]).then_inc(s_outd[i % 2], 16)
                        w = min(b, tail) - a
                        if w > 0:
                            sp.dma_start(ov[full * HI * D + a:full * HI * D + a + w].rearrange("(o f) -> o f", o=1), o[full:full + 1, 0:w]).then_inc(s_outd[i % 2], 16)
            for i in (PIECES - 2, PIECES - 1):
                sp.wait_ge(s_outd[i % 2], stored(i))

        @block.gpsimd
        def _(pool):
            pool.iota(iota[:, :], [[1, HI]], base=0, channel_multiplier=0, allow_small_or_imprecise_dtypes=True).then_inc(s_const, 1)
            pool.iota(pid[:, :], [[0, 1]], base=0, channel_multiplier=1, allow_small_or_imprecise_dtypes=True).then_inc(s_const, 1)
            pool.iota(trash[:, :], [[0, 1]], base=NP, channel_multiplier=1, allow_small_or_imprecise_dtypes=True).then_inc(s_const, 1)
            pool.memset(ident[:, :], 0.0).then_inc(s_const, 1)
            pool.memset(earlier[:, :], 1.0).then_inc(s_const, 1)
            pool.memset(zero[:, :], 0.0).then_inc(s_const, 1)
            pool.memset(eps[:, 0:1], EPS_LN).then_inc(s_const, 1)
            pool.memset(eps[:, 1:2], EPS_DEG).then_inc(s_const, 1)
            pool.wait_ge(s_const, 8)
            pool.affine_select(out=ident[:, :], in_=ident[:, :], compare_op=ALU.not_equal, fill=1.0, base=0,
                               pattern=[[-1, P]], channel_multiplier=1).then_inc(s_const, 1)
            pool.affine_select(out=earlier[:, :], in_=earlier[:, :], compare_op=ALU.is_gt, fill=0.0, base=0,
                               pattern=[[-1, P]], channel_multiplier=1).then_inc(s_const, 1)
            for L in range(2):
                base = L * NS
                pool.wait_ge(s_yd, 16 * (L + 1))
                pool.wait_ge(s_zero[L], 16 * CH * 8)

                def body(i):
                    for h in range(2):
                        t = i * 2 + h
                        pool.wait_ge(s_idx, base + t + 1)
                        wait(pool, s_pm, base + t - 1)
                        pool.nop(nofuse=True)
                        for k in range(CH):
                            pool.indirect_dma_start(
                                out=G[:, h, k, :], out_offset=None, in_=y_d[L],
                                in_offset=bass.IndirectOffsetOnAxis(ap=cidx[:, h, k:k + 1], axis=0)).then_inc(s_gat[h], 16)
                        pool.wait_ge(s_mo, base + t + 1)
                        for k in range(CH):
                            wait(pool, s_tab[k], (base + t) * 16)
                            pool.nop(nofuse=True)
                            pool.indirect_dma_start(
                                out=tab_d[L][k], out_offset=bass.IndirectOffsetOnAxis(ap=ridx[:, h, k:k + 1], axis=0),
                                in_=Mo[:, h, k, :], in_offset=None, compute_op=ALU.add).then_inc(s_tab[k], 16)
                steps(pool, NS // 2, body)
            for k in range(CH):
                pool.wait_ge(s_tab[k], 16 * NS * 2)

        @block.scalar
        def _(act):
            def clear_tables(L):
                for k in range(CH):
                    t = tab_d[L][k].rearrange("(p r) d -> p (r d)", p=P)
                    for i in range(8):
                        act.dma_start(t[:, i * ZW:(i + 1) * ZW], zero[:, :]).then_inc(s_zero[L], 16)
            act.wait_ge(s_const, 8)
            clear_tables(0)
            act.wait_ge(s_v2a, 1)
            act.activation(logit[:, :], ga[:, :], ACT.Ln).then_inc(s_a2v, 1)
            act.activation(gb[:, :], ga[:, :], ACT.Ln, bias=1.0, scale=-1.0).then_inc(s_a2v, 1)
            for p_ in range(PIECES):
                act.wait_ge(s_v2a, 2 + p_)
                act.activation(st[:, 1, :], st[:, 0, :], ACT.Sqrt, bias=eps[:, 0:1], scale=1.0 / D).then_inc(s_a2v, 1)
            act.wait_ge(s_w, 16 * 14)
            for L in range(2):
                base = L * NS

                def node_group(g, slot):
                    n = L * NG + g
                    hT = Z[0:D, slot * 384:(slot + 1) * 384]
                    rT = Z[:, 768 + slot * 384:768 + (slot + 1) * 384]
                    act.wait_ge(s_T, n + 1)
                    act.activation(hT, psG[0:D, slot, 0:384], ACT.Copy).then_inc(s_hT, 1)
                    act.wait_ge(s_mm, n + 1)
                    wait(act, s_sm, n - 1)
                    act.activation(rT, psG[:, 2 + slot, 0:384], ACT.Relu, bias=bias[L][:, 0:1]).then_inc(s_rT, 1)

                def pair(i):
                    for s in range(2):
                        node_group(i * 2 + s, s)
                steps(act, NG // 2, pair)
                node_group(NG - 1, 0)
                act.wait_ge(s_v2a, 2 + PIECES + 2 * L)
                act.activation(gb[:, :], ga[:, :], ACT.Sigmoid).then_inc(s_a2v, 1)
                act.wait_ge(s_v2a, 3 + PIECES + 2 * L)
                act.activation(dinv[:, :], abr[:, 0, :], ACT.Sqrt).then_inc(s_a2v, 1)
                if L == 0:
                    clear_tables(1)

                def body(i):
                    for h in range(2):
                        t = i * 2 + h
                        act.wait_ge(s_pm, base + t + 1)
                        for k in range(CH):
                            wait(act, s_tab[k], (base + t - 1) * 16)
                        act.activation(Mo[:, h, :, :].rearrange("p k d -> p (k d)"), psG[:, h, :], ACT.Copy).then_inc(s_mo, 1)
                steps(act, NS // 2, body)

        @block.vector
        def _(dve):
            chained = [0]

            def link(ins):
                chained[0] += 1
                ins.then_inc(s_dve, 1)
                dve.wait_ge(s_dve, chained[0])

            dve.memset(A[0].bitcast(i32), PAD_ROW).then_inc(s_pad, 1)
            dve.memset(A[1].bitcast(i32), N - 1).then_inc(s_pad, 1)
            dve.memset(A[2], 0.5).then_inc(s_pad, 1)
            dve.memset(att[0][:, :], 0.0)
            dve.memset(att[1][:, :], 0.0).then_inc(s_pad, 1)

            def split(a, q, r):
                link(dve.tensor_scalar(q.bitcast(i32), a, 1.0 / HI, None, ALU.mult))
                link(dve.tensor_copy(q, q.bitcast(i32)))
                link(dve.scalar_tensor_tensor(r, q, -float(HI), a, ALU.mult, ALU.add))
                link(dve.scalar_tensor_tensor(q, r, 0.0, q, ALU.is_lt, ALU.subtract))
                link(dve.scalar_tensor_tensor(q, r, float(HI), q, ALU.is_ge, ALU.subtract))
                link(dve.scalar_tensor_tensor(a, q, -float(HI), a, ALU.mult, ALU.add))

            dve.wait_ge(s_row, 48)
            link(dve.tensor_copy(A[0], A[0].bitcast(i32)))
            dve.tensor_copy(U[0], A[0]).then_inc(s_u16, 1)
            split(A[0], B[0], B[2])
            dve.tensor_copy(U[1], B[0]).then_inc(s_u16, 1)
            dve.wait_ge(s_col, 48)
            link(dve.tensor_copy(A[1], A[1].bitcast(i32)))
            split(A[1], B[1], B[2])
            dve.tensor_copy(U[2], B[1]).then_inc(s_u16, 1)
            dve.wait_ge(s_nz, 48)
            dve.tensor_copy(B[2][:, 0:1], B[2][:, 0:1]).then_inc(s_split, 1)
            dest = [lof, hif, rowf, chif, gb]
            n = 0
            for a, d in enumerate(dest):
                dv = d[:, :].rearrange("q (p j k) -> q j k p", j=RJ, k=CH)
                for j in range(RJ):
                    for kk in range(2):
                        dve.wait_ge(s_tp, n + 1)
                        if a == 4 and j == 0 and kk == 0:
                            dve.wait_ge(s_scr, 48)
                        dve.tensor_copy(dv[:, j, 4 * kk:4 * kk + 4, :],
                                        psG[:, n % 6, 0:4 * RP].rearrange("q (k p) -> q k p", k=4)).then_inc(s_tpe, 1)
                        n += 1
            dve.wait_ge(s_tpe, n)
            link(dve.scalar_tensor_tensor(coli[:, :], rowf[:, :], float(HI), chif[:, :], ALU.mult, ALU.add))
            link(dve.scalar_tensor_tensor(rowf[:, :], lof[:, :], float(HI), hif[:, :], ALU.mult, ALU.add))
            dve.tensor_scalar(ga[:, :], gb[:, :], EPS_NOISE, 1.0 - EPS_NOISE, ALU.max, ALU.min).then_inc(s_v2a, 1)
            dve.wait_ge(s_a2v, 2)
            link(dve.tensor_tensor(logit[:, :], logit[:, :], gb[:, :], ALU.subtract))
            link(dve.memset(cur[96:P, :], 0.0))
            dve.sem_inc(s_split, 3)
            dve.wait_ge(s_x, 48)
            dve.wait_ge(s_const, 10)
            for p_ in range(PIECES):
                def piece(t):
                    return t[:, p_ * PW:(p_ + 1) * PW].rearrange("p (h d) -> p h d", d=D)
                sq = Z[:, 0:PW].rearrange("p (h d) -> p h d", d=D)
                s0, s1 = st[:, 0, :], st[:, 1, :]
                link(dve.tensor_reduce(s0, piece(cur), AX.X, ALU.add))
                link(dve.tensor_scalar(s1, s0, 1.0 / D, None, ALU.mult))
                link(dve.tensor_tensor(piece(work), piece(cur), s1.unsqueeze(2).to_broadcast([P, PH, D]), ALU.subtract))
                link(dve.tensor_tensor(sq, piece(work), piece(work), ALU.mult))
                dve.tensor_reduce(s0, sq, AX.X, ALU.add).then_inc(s_v2a, 1)
                dve.wait_ge(s_a2v, 3 + p_)
                link(dve.reciprocal(s0, s1))
                link(dve.tensor_tensor(piece(work), piece(work), s0.unsqueeze(2).to_broadcast([P, PH, D]), ALU.mult))
                link(dve.tensor_scalar(piece(work), piece(work), 0.0, None, ALU.max))
                link(dve.tensor_tensor(piece(cur), piece(cur), piece(work), ALU.add))
            dve.sem_inc(s_acc, 1)

            for L in range(2):
                base = L * NS

                def stage(g, slot):
                    wait(dve, s_T, L * NG + g - 1)
                    dve.tensor_copy(Xs[:, slot, :], X[L][:, bass.ds(g * (GH * D), GH * D)]).then_inc(s_stg, 1)

                def node_group(g, slot):
                    n = L * NG + g
                    dve.wait_ge(s_sm, n + 1)
                    dve.tensor_copy(ab[:, bass.ds(g * GH, GH), :], psG[:, 4 + slot, 0:2 * GH].rearrange("p (h t) -> p h t", t=2)).then_inc(s_ab, 1)

                def pair(i):
                    for s in range(2):
                        stage(i * 2 + s, s)
                    for s in range(2):
                        node_group(i * 2 + s, s)
                steps(dve, NG // 2, pair)
                stage(NG - 1, 0)
                node_group(NG - 1, 0)
                dve.wait_ge(s_ab, NG * (L + 1))
                abv = ab[:, :, :].rearrange("p h t -> p t h")
                link(dve.tensor_copy(abs3[:, 0, :, :], abv))
                link(dve.tensor_tensor(abr[:, :, :], abv, abs3[:, 0, :, :], ALU.subtract))
                link(dve.tensor_copy(abs3[:, 1, :, :], abr[:, :, :]))
                link(dve.tensor_tensor(abr[:, :, :], abr[:, :, :], abs3[:, 1, :, :], ALU.subtract))
                dve.tensor_copy(abs3[:, 2, :, :], abr[:, :, :]).then_inc(s_abs, 1)

                def one_hot(t, i):
                    dve.wait_ge(s_lo[t], (base + i + 1) * 16)
                    wait(dve, s_g[t], base + i)
                    dve.tensor_scalar(ones_lo[:, t, :], lo_bc[:, t, :], pid[:, 0:1], None, ALU.is_equal).then_inc(s_oh[t], 1)

                def select(t, i):
                    dve.wait_ge(s_g[t], base + i + 1)
                    wait(dve, s_sel[t], base + i)
                    for k in range(CH):
                        c = i * CH + k
                        ins = dve.scalar_tensor_tensor(
                            junk[t][:, k, :], iota[:, :], (hif, chif)[t][:, bass.ds(c, 1)],
                            psG[:, 3 * t + k // 3, (k % 3) * HI:(k % 3 + 1) * HI], ALU.is_equal, ALU.mult,
                            accum_out=(ga, gb)[t][:, bass.ds(c, 1)])
                    ins.then_inc(s_sel[t], 1)

                def gather(i, last=False):
                    one_hot(1, i)
                    select(0, i)
                    if not last:
                        one_hot(0, i + 1)
                    select(1, i)
                one_hot(0, 0)
                with dve.Fori(0, NS - 1) as i:
                    gather(i)
                gather(NS - 1, True)
                dve.wait_ge(s_sel[1], base + NS)
                link(dve.scalar_tensor_tensor(ga[:, :], ga[:, :], attb[L][:, 0:1], gb[:, :], ALU.add, ALU.add))
                dve.tensor_tensor(ga[:, :], ga[:, :], logit[:, :], ALU.add).then_inc(s_v2a, 1)
                dve.wait_ge(s_a2v, 3 + PIECES + 2 * L)
                link(dve.tensor_scalar(ga[:, :], gb[:, :], ZETA - GAMMA, GAMMA, ALU.mult, ALU.add))
                link(dve.tensor_scalar(ga[:, :], ga[:, :], 0.0, 1.0, ALU.max, ALU.min))

                def scatter(i):
                    for k in range(CH):
                        n = (base + i) * CH + k
                        c = i * CH + k
                        wait(dve, s_acm, n - CH + 1)
                        dve.tensor_scalar(OA[:, k, :], iota[:, 0:P], lof[:, bass.ds(c, 1)], ga[:, bass.ds(c, 1)], ALU.is_equal, ALU.mult)
                        dve.tensor_scalar(OB[:, k, :], iota[:, :], hif[:, bass.ds(c, 1)], None, ALU.is_equal).then_inc(s_oab, 1)
                steps(dve, NS, scatter)
                dve.wait_ge(s_R, L + 1)
                dve.tensor_scalar(abr[:, 0, :], psR[:, 0:HI], EPS_DEG, None, ALU.add).then_inc(s_v2a, 1)
                dve.wait_ge(s_a2v, 4 + PIECES + 2 * L)
                link(dve.reciprocal(abr[:, 1, :], dinv[:, :]))
                link(dve.tensor_scalar(dinv[:, :], abr[:, 1, :], 0.0, 10.0, ALU.max, ALU.min))
                if L == 0:
                    dve.wait_ge(s_accd, 16)
                dve.tensor_tensor(Y[L][:, :].rearrange("p (h d) -> p h d", d=D), X[L][:, :].rearrange("p (h d) -> p h d", d=D),
                                  dinv[:, :].unsqueeze(2).to_broadcast([P, HI, D]), ALU.mult).then_inc(s_y, 1)

                def body(i):
                    for h in range(2):
                        t = i * 2 + h
                        c = t * CH
                        wait(dve, s_idx, base + t)
                        dve.wait_ge(s_rb[h], ((base // 2) + i + 1) * 16)
                        for k in range(CH):
                            dve.scalar_tensor_tensor(junk2[:, k, :], row_bc[:, h, k * P:(k + 1) * P], rowf[:, bass.ds(c + k, 1)],
                                                     earlier[:, :], ALU.is_equal, ALU.mult, accum_out=cnt[:, k:k + 1])
                        for k in range(CH):
                            wait(dve, s_tab[k], (base + t - 1) * 16)
                        dve.tensor_copy(cidx[:, h, :], coli[:, bass.ds(c, CH)])
                        dve.tensor_scalar(dtmp[:, :], rowf[:, bass.ds(c, CH)], -1.0, trash[:, 0:1], ALU.mult, ALU.add).then_inc(s_cnt, 1)
                        dve.wait_ge(s_cnt, (base + t) * 2 + 1)
                        dve.scalar_tensor_tensor(dtmp[:, :], cnt[:, :], 1.0, dtmp[:, :], ALU.min, ALU.mult).then_inc(s_cnt, 1)
                        dve.wait_ge(s_cnt, (base + t) * 2 + 2)
                        dve.tensor_tensor(ridx[:, h, :], dtmp[:, :], rowf[:, bass.ds(c, CH)], ALU.add).then_inc(s_idx, 1)
                        wait(dve, s_pm, base + t - 1)
                        for k in range(CH):
                            ins = dve.tensor_scalar(Sw[:, h, k, :], row_bc[:, h, k * P:(k + 1) * P], rowf[:, bass.ds(c + k, 1)],
                                                    ga[:, bass.ds(c + k, 1)], ALU.is_equal, ALU.mult)
                        ins.then_inc(s_sw, 1)
                steps(dve, NS // 2, body)

                parts = CH + L
                before = 0 if L == 0 else PIECES * CH
                for p_ in range(PIECES):
                    S = work[:, (2 + p_ % 2) * PW:(3 + p_ % 2) * PW]
                    if L == 1 and p_ >= 2:
                        dve.wait_ge(s_outd[p_ % 2], stored(p_ - 2))
                    for k in range(parts):
                        n = before + p_ * parts + k
                        dve.wait_ge(s_tl[n % 2], 16 * (n // 2 + 1))
                        T = work[:, (n % 2) * PW:(n % 2 + 1) * PW]
                        if k == 0:
                            ins = dve.tensor_copy(S, T)
                        else:
                            ins = dve.tensor_tensor(S, S, T, ALU.add)
                        ins.then_inc(s_add, 1)
                        dve.wait_ge(s_add, n + 1)
                        if k == CH - 1:
                            Sv = S.rearrange("p (h d) -> p h d", d=D)
                            dv = dinv[:, p_ * PH:(p_ + 1) * PH].unsqueeze(2).to_broadcast([P, PH, D])
                            C = cur[:, p_ * PW:(p_ + 1) * PW]
                            if L == 0:
                                link(dve.tensor_tensor(C.rearrange("p (h d) -> p h d", d=D), Sv, dv, ALU.mult))
                            else:
                                link(dve.tensor_tensor(Sv, Sv, dv, ALU.mult))
                                link(dve.tensor_tensor(S, S, C, ALU.add))
                    if L == 1:
                        dve.sem_inc(s_piece, 1)

        @block.tensor
        def _(pe):
            pe.wait_ge(s_const, 10)
            n = 0
            pe.wait_ge(s_split, 1)
            for a in (B[0], A[0], B[1], A[1], A[2]):
                for j in range(RJ):
                    for kk in range(2):
                        if n >= 6:
                            pe.wait_ge(s_tpe, n - 5)
                        for k in range(4):
                            f = (j * CH + kk * 4 + k) * P
                            ins = pe.transpose(psG[:, n % 6, k * RP:(k + 1) * RP], a[:, f:f + P], ident[0:RP, 0:RP])
                        ins.then_inc(s_tp, 1)
                        n += 1
            pe.wait_ge(s_w, 16 * 14)
            for L in range(2):
                base = L * NS

                def pair(i, slots=2):
                    for s in range(slots):
                        g = i * 2 + s
                        pe.wait_ge(s_stg, L * NG + g + 1)
                        pe.nop(nofuse=True)
                        for b in range(GH):
                            ins = pe.transpose(psG[0:D, s, b * P:(b + 1) * P], Xs[:, s, b * D:(b + 1) * D], ident[:, :])
                        ins.then_inc(s_T, 1)
                    for s in range(slots):
                        n = L * NG + i * 2 + s
                        pe.wait_ge(s_hT, n + 1)
                        wait(pe, s_rT, n - 1)
                        pe.matmul(psG[:, 2 + s, 0:384], W[L][:, :], Z[0:D, s * 384:(s + 1) * 384], start=True, stop=True).then_inc(s_mm, 1)
                    for s in range(slots):
                        n = L * NG + i * 2 + s
                        pe.wait_ge(s_rT, n + 1)
                        wait(pe, s_ab, n - 1)
                        rT = Z[:, 768 + s * 384:768 + (s + 1) * 384]
                        for b in range(GH):
                            ins = pe.matmul(psG[:, 4 + s, 2 * b:2 * b + 2], rT[:, b * P:(b + 1) * P], att[L][:, :], start=True, stop=True)
                        ins.then_inc(s_sm, 1)
                steps(pe, NG // 2, pair)
                pair(NG // 2, 1)

                pe.wait_ge(s_abs, L + 1)

                def gather(i):
                    for t in range(2):
                        pe.wait_ge(s_oh[t], base + i + 1)
                        wait(pe, s_sel[t], base + i)
                        for k in range(CH):
                            for m in range(3):
                                ins = pe.matmul(psG[:, 3 * t + k // 3, (k % 3) * HI:(k % 3 + 1) * HI],
                                                ones_lo[:, t, k * P:(k + 1) * P], abs3[:, m, t, :], start=m == 0, stop=m == 2)
                        ins.then_inc(s_g[t], 1)
                steps(pe, NS, gather)

                pe.matmul(psR[:, 0:HI], zero[:, 0:P], zero[:, 0:HI], start=True, stop=False)

                def scatter(i):
                    for k in range(CH):
                        pe.wait_ge(s_oab, (base + i) * CH + k + 1)
                        pe.matmul(psR[:, 0:HI], OA[:, k, :], OB[:, k, :], start=False, stop=False).then_inc(s_acm, 1)
                steps(pe, NS, scatter)
                pe.matmul(psR[:, 0:HI], zero[:, 0:P], zero[:, 0:HI], start=False, stop=True).then_inc(s_R, 1)

                def body(i):
                    for h in range(2):
                        t = i * 2 + h
                        pe.wait_ge(s_sw, base + t + 1)
                        pe.wait_ge(s_gat[h], (base // 2 + i + 1) * 16 * CH)
                        wait(pe, s_mo, base + t - 1)
                        for k in range(CH):
                            ins = pe.matmul(psG[:, h, k * D:(k + 1) * D], Sw[:, h, k, :], G[:, h, k, :], start=True, stop=True)
                        ins.then_inc(s_pm, 1)
                steps(pe, NS // 2, body)


_PARAMS = ['nbW', 'nbb', 'selfW', 'selfb', 'attW', 'attb']
_INS = ['x', 'src', 'dst', 'edge_weight1'] + [f'L0_gnn_{p}{L}' for L in range(2) for p in _PARAMS]


def kernel(**inputs):
    import numpy as _np
    import concourse.bacc as _bacc
    from concourse import mybir as _mybir
    from concourse.bass_utils import run_bass_kernel_spmd as _run
    nc = _bacc.Bacc("TRN2", target_bir_lowering=False, num_devices=1)
    arrays, args = {}, []
    for name in _INS:
        a = _np.ascontiguousarray(inputs[name])
        arrays[f"in_{name}_dram"] = a
        args.append(nc.dram_tensor(f"in_{name}_dram", a.shape, _mybir.dt.from_np(a.dtype), kind="ExternalInput").ap())
    out = nc.dram_tensor("out_0_dram", (N, D), _mybir.dt.float32, kind="ExternalOutput").ap()
    build(nc, *args[:4], [args[4:10], args[10:16]], out)
    r = _run(nc, [arrays], core_ids=[0])
    return r.results[0]["out_0_dram"]
```

```python
import concourse.bass as bass
from concourse import mybir
from contextlib import ExitStack

N, D, E = 18750, 64, 318750
P = 128
HI = -(-N // P)
NP = P * HI
CH = 8
SE = CH * P
RJ = 3
RP = -(-E // (SE * RJ))
NS = RP * RJ
NC = NS * CH
RW = RJ * SE
EP = NS * SE
PAD_ROW = NP
TABLE_ROWS = NP + P
GAMMA, ZETA = -0.45, 1.05
EPS_NOISE, EPS_DEG, EPS_LN = 1e-7, 1e-6, 1e-5
PIECES = 7
PH = HI // PIECES
PW = PH * D
ZW = TABLE_ROWS * D // P // 8
GH = 3
NG = HI // GH
assert HI % PIECES == 0 and HI % GH == 0 and NG % 2 == 1 and NS % 2 == 0


def build(nc, x, src, dst, noise, params, out):
    f32, bf16, i32, u16 = mybir.dt.float32, mybir.dt.bfloat16, mybir.dt.int32, mybir.dt.uint16
    ALU, ACT, AX = mybir.AluOpType, mybir.ActivationFunctionType, mybir.AxisListType

    row_d = nc.dram_tensor("row_d", (EP,), u16).ap()
    rlo_d = nc.dram_tensor("rlo_d", (EP,), u16).ap()
    crel_d = nc.dram_tensor("crel_d", (EP,), u16).ap()
    base_d = nc.dram_tensor("base_d", (NS,), i32).ap()
    b_d = [nc.dram_tensor(f"b_d{L}", (NP, 1), f32).ap() for L in range(2)]
    clo_d = nc.dram_tensor("clo_d", (EP,), u16).ap()
    acc_d = nc.dram_tensor("acc_d", (P, HI * D), f32).ap()
    y_d = [nc.dram_tensor(f"y_d{L}", (NP, D), f32).ap() for L in range(2)]
    tab_d = [[nc.dram_tensor(f"tab_d{L}_{k}", (TABLE_ROWS, D), f32).ap() for k in range(CH)] for L in range(2)]

    ctx = ExitStack()
    with ctx:
        def sb(name, shape, dt):
            return ctx.enter_context(nc.sbuf_tensor(name, shape, dt))

        def sem(name):
            return ctx.enter_context(nc.semaphore(name))

        cur = sb("cur", [P, HI * D], f32)
        work = sb("work", [P, HI * D], f32)
        rowf = sb("rowf", [P, NC], f32)
        lof = sb("lof", [P, NC], f32)
        hif = sb("hif", [P, NC], f32)
        chif = sb("chif", [P, NC], f32)
        coli = sb("coli", [P, NC], i32)
        logit = sb("logit", [P, NC], f32)
        ga = sb("ga", [P, NC], f32)
        gb = sb("gb", [P, NC], f32)
        ones_lo = sb("ones_lo", [P, 2, SE], bf16)
        lo_bc = sb("lo_bc", [P, 2, SE], u16)
        row_bc = sb("row_bc", [P, 2, SE], u16)
        Z = sb("Z", [P, CH * (P + HI)], f32)
        G = sb("G", [P, 2, CH, D], f32)
        Sw = sb("Sw", [P, 2, CH, P], f32)
        Mo = sb("Mo", [P, 2, CH, D], f32)
        zero = sb("zero", [P, ZW], f32)
        iota = sb("iota", [P, HI], f32)
        pid = sb("pid", [P, 1], f32)
        trash = sb("trash", [P, 1], f32)
        ident = sb("ident", [P, P], f32)
        earlier = sb("earlier", [P, P], f32)
        W = [sb(f"W{L}", [D, 2 * D], f32) for L in range(2)]
        bias = [sb(f"bias{L}", [P, 1], f32) for L in range(2)]
        att = [sb(f"att{L}", [P, 2], f32) for L in range(2)]
        attb = [sb(f"attb{L}", [P, 1], f32) for L in range(2)]
        ab = sb("ab", [P, HI, 2], f32)
        abs3 = sb("abs3", [P, 3, 2, HI], bf16)
        abr = sb("abr", [P, 2, HI], f32)
        st = sb("st", [P, 2, PH], f32)
        eps = sb("eps", [P, 2], f32)
        dinv = sb("dinv", [P, HI], f32)
        ridx = sb("ridx", [P, 2, CH], i32)
        cidx = sb("cidx", [P, 2, CH], i32)
        cnt = sb("cnt", [P, CH], f32)
        dtmp = sb("dtmp", [P, CH], f32)
        psG = ctx.enter_context(nc.psum_tensor("psG", [P, 6, 512], f32))
        psR = ctx.enter_context(nc.psum_tensor("psR", [P, 2, 512], f32))
        bt = sb("bt", [P, HI], f32)
        bw = sb("bw", [P, 2], f32)
        yw = sb("yw", [P, 2, D], f32)
        bases = sb("bases", [1, NS], i32)
        span = sb("span", [P, 3, RJ], f32)
        wide = sb("wide", [P, 2], f32)
        local = sb("local", [P, 1], i32)
        OC = Z[:, 0:2 * SE].rearrange("p (h n) -> p h n", h=2)
        junk = [t.rearrange("p (k n) -> p k n", k=CH) for t in
                (Sw[:, :, :, :].rearrange("p a k n -> p (a k n)")[:, 0:CH * HI], Z[:, 0:CH * HI])]
        junk2 = sb("junk2", [P, CH, P], f32)
        Xs = Z[:, 1536:1536 + 2 * GH * D].rearrange("p (s n) -> p s n", s=2)
        X = [work, cur]
        Y = [cur, work]
        A = [work[0:RP, i * RW:(i + 1) * RW] for i in range(3)]
        B = [cur[0:RP, i * RW:(i + 1) * RW] for i in range(3)]
        U = [t[0:RP, 0:RW // 2].bitcast(u16) for t in (logit, ga, gb, rowf)]
        OB = [t[:, 0:2 * CH * HI].rearrange("p (h k n) -> p h k n", h=2, k=CH) for t in Y]
        OAw = [t[:, 2400:2400 + 2 * SE].rearrange("p (h k n) -> p h k n", h=2, k=CH) for t in Y]
        OA = [t[:, 4480:4480 + SE].bitcast(bf16).rearrange("p (h k n) -> p h k n", h=2, k=CH) for t in Y]

        s_pad, s_const, s_w, s_x = sem("s_pad"), sem("s_const"), sem("s_w"), sem("s_x")
        s_row, s_col, s_nz = sem("s_row"), sem("s_col"), sem("s_nz")
        s_u16, s_scr = sem("s_u16"), sem("s_scr")
        s_split, s_tp, s_tpe = sem("s_split"), sem("s_tp"), sem("s_tpe")
        s_dve, s_v2a, s_a2v = sem("s_dve"), sem("s_v2a"), sem("s_a2v")
        s_acc, s_accd = sem("s_acc"), sem("s_accd")
        s_stg = sem("s_stg")
        s_T, s_hT, s_mm, s_rT, s_sm, s_ab = (sem(n) for n in ("s_T", "s_hT", "s_mm", "s_rT", "s_sm", "s_ab"))
        s_abs, s_mask = sem("s_abs"), sem("s_mask")
        s_lo = [sem("s_lo_r"), sem("s_lo_c")]
        s_oh = [sem("s_oh_r"), sem("s_oh_c")]
        s_g = [sem("s_g_r"), sem("s_g_c")]
        s_sel = [sem("s_sel_r"), sem("s_sel_c")]
        s_ob = sem("s_ob")
        s_oab, s_acm, s_R = sem("s_oab"), sem("s_acm"), sem("s_R")
        s_y, s_yd = sem("s_y"), sem("s_yd")
        s_oaw = sem("s_oaw")
        s_span, s_wide, s_local, s_basd, s_bases, s_bt, s_btd = (sem(n) for n in ("s_span", "s_wide", "s_local", "s_basd", "s_bases", "s_bt", "s_btd"))
        s_rl, s_cb, s_bw, s_cb2, s_yw = ([sem(f"{n}{h}") for h in range(2)] for n in ("s_rl", "s_cb", "s_bw", "s_cb2", "s_yw"))
        s_oc, s_ge, s_gev = sem("s_oc"), sem("s_ge"), sem("s_gev")
        s_zero = [sem("s_zero0"), sem("s_zero1")]
        s_rb = [sem("s_rb0"), sem("s_rb1")]
        s_cnt, s_idx, s_sw, s_pm, s_mo = (sem(n) for n in ("s_cnt", "s_idx", "s_sw", "s_pm", "s_mo"))
        s_gat = [sem("s_gat0"), sem("s_gat1")]
        s_tab = [sem(f"s_tab{k}") for k in range(CH)]
        s_tl = [sem("s_tl0"), sem("s_tl1")]
        s_add, s_piece, s_outd = sem("s_add"), sem("s_piece"), [sem("s_outd0"), sem("s_outd1")]

        def wait(eng, semaphore, value):
            if not isinstance(value, int) or value > 0:
                eng.wait_ge(semaphore, value)

        def steps(eng, n, body):
            body(0)
            with eng.Fori(1, n - 1) as i:
                body(i)
            body(n - 1)

        def rows_dma(eng, dram, tile, width, total, semaphore):
            full = total // width
            cut = full // 16 * 16
            for a, b in ((0, cut), (cut, full)):
                eng.dma_start(tile[a:b, 0:width], dram[a * width:b * width].rearrange("(p f) -> p f", f=width)).then_inc(semaphore, 16)
            rest = total - full * width
            eng.dma_start(tile[full:full + 1, 0:rest], dram[full * width:total].rearrange("(p f) -> p f", p=1)).then_inc(semaphore, 16)

        def stored(i):
            tail = (N - N // HI * HI) * D
            return 16 * sum(2 + (j * PW < tail) for j in range(i % 2, i + 1, 2))

        xv = x.rearrange("n d -> (n d)")
        block = ctx.enter_context(nc.Block())

        @block.sync
        def _(sp):
            sp.wait_ge(s_pad, 1)
            rows_dma(sp, src, A[0].bitcast(i32), RW, E, s_row)
            sp.wait_ge(s_pad, 2)
            rows_dma(sp, dst, A[1].bitcast(i32), RW, E, s_col)
            sp.wait_ge(s_pad, 3)
            rows_dma(sp, noise.rearrange("e o -> (e o)"), A[2], RW, E, s_nz)
            for L, (nbW, nbb, selfW, selfb, attW, attbias) in enumerate(params):
                sp.dma_start(W[L][:, 0:D], nbW).then_inc(s_w, 16)
                sp.dma_start(W[L][:, D:2 * D], selfW).then_inc(s_w, 16)
                sp.dma_start(bias[L][0:D, :], nbb.rearrange("(d o) -> d o", o=1)).then_inc(s_w, 16)
                sp.dma_start(bias[L][D:P, :], selfb.rearrange("(d o) -> d o", o=1)).then_inc(s_w, 16)
                sp.wait_ge(s_pad, 4)
                sp.dma_start(att[L][0:D, 0:1], attW[0:D, :]).then_inc(s_w, 16)
                sp.dma_start(att[L][D:P, 1:2], attW[D:2 * D, :]).then_inc(s_w, 16)
                sp.dma_start(attb[L][:, :], attbias.rearrange("(a o) -> a o", o=1).to_broadcast([P, 1])).then_inc(s_w, 16)
            for n, (d, u) in enumerate(((row_d, U[0]), (rlo_d, U[1]), (crel_d, U[3]), (clo_d, U[2]))):
                sp.wait_ge(s_u16, n + 1)
                sp.dma_start(d.rearrange("(p f) -> p f", p=RP), u).then_inc(s_scr, 16)
            sp.wait_ge(s_span, 1)
            sp.dma_start(base_d.rearrange("(p j) -> p j", p=RP), span[0:RP, 2, :].bitcast(i32)).then_inc(s_basd, 16)
            sp.wait_ge(s_basd, 16)
            sp.dma_start(bases[:, :], base_d.rearrange("(o n) -> o n", o=1)).then_inc(s_bases, 16)
            sp.wait_ge(s_split, 4)
            rows_dma(sp, xv, cur, HI * D, N * D, s_x)
            sp.wait_ge(s_acc, 1)
            sp.dma_start(acc_d, cur[:, :]).then_inc(s_accd, 16)
            sp.wait_ge(s_scr, 64)
            sp.wait_ge(s_bases, 16)
            sp.wait_ge(s_local, 1)
            is_local = sp.value_load(local[0:1, 0:1], min_val=0, max_val=1)

            def window(t):
                return sp.value_load(bases[0:1, bass.ds(t, 1)], min_val=0, max_val=NP - P)

            def spread(d, t):
                return d[bass.ds(t * SE, SE)].rearrange("(o f) -> o f", o=1).to_broadcast([P, SE])

            for L in range(2):
                base = L * NS
                sp.wait_ge(s_bt, L + 1)
                sp.dma_start(b_d[L].rearrange("(p f) o -> p (f o)", p=P), bt[:, :]).then_inc(s_btd, 16)
                sp.wait_ge(s_btd, 16 * (L + 1))

                def load_lo(i):
                    for t, d in enumerate((rlo_d, clo_d)):
                        wait(sp, s_oh[t], base + i)
                        sp.dma_start(lo_bc[:, t, :], d[bass.ds(i * SE, SE)].rearrange("(o f) -> o f", o=1).to_broadcast([P, SE])).then_inc(s_lo[t], 16)

                def load_lo_local(i):
                    for h in range(2):
                        t = i * 2 + h
                        wait(sp, s_oh[0], base + t - 1)
                        sp.dma_start(lo_bc[:, h, :], spread(rlo_d, t)).then_inc(s_rl[h], 16)
                        wait(sp, s_oh[1], base + t - 1)
                        sp.dma_start(row_bc[:, h, :], spread(crel_d, t)).then_inc(s_cb[h], 16)
                        wait(sp, s_g[1], base + t - 1)
                        sp.dma_start(bw[:, h:h + 1], b_d[L][bass.ds(window(t), P), :]).then_inc(s_bw[h], 16)
                with sp.If(is_local):
                    steps(sp, NS // 2, load_lo_local)
                with sp.Else():
                    steps(sp, NS, load_lo)
                sp.wait_ge(s_y, L + 1)
                sp.dma_start(y_d[L].rearrange("(p f) d -> p (f d)", p=P), Y[L][:, :]).then_inc(s_yd, 16)

                def load_row(i):
                    for h in range(2):
                        wait(sp, s_sw, base + i * 2 + h - 1)
                        sp.dma_start(row_bc[:, h, :], row_d[bass.ds((i * 2 + h) * SE, SE)].rearrange("(o f) -> o f", o=1).to_broadcast([P, SE])).then_inc(s_rb[h], 16)

                def load_row_local(i):
                    for h in range(2):
                        t = i * 2 + h
                        wait(sp, s_sw, base + t - 1)
                        sp.dma_start(row_bc[:, h, :], spread(row_d, t)).then_inc(s_rb[h], 16)
                        wait(sp, s_oc, base + t - 1)
                        sp.dma_start(lo_bc[:, h, :], spread(crel_d, t)).then_inc(s_cb2[h], 16)
                        wait(sp, s_ge, base + t - 1)
                        sp.dma_start(yw[:, h, :], y_d[L][bass.ds(window(t), P), :]).then_inc(s_yw[h], 16)
                sp.wait_ge(s_yd, 16 * (L + 1))
                with sp.If(is_local):
                    steps(sp, NS // 2, load_row_local)
                with sp.Else():
                    steps(sp, NS // 2, load_row)
                for k in range(CH):
                    sp.wait_ge(s_tab[k], 16 * NS * (L + 1))
                sp.wait_ge(s_yd, 16 * (L + 1))
                srcs = [tab_d[L][k][0:NP, :].rearrange("(p f) d -> p (f d)", p=P) for k in range(CH)] + [acc_d] * L
                before = 0 if L == 0 else PIECES * CH
                for i in range(PIECES):
                    for k, s_ in enumerate(srcs):
                        n = before + i * len(srcs) + k
                        if n >= before + 2:
                            sp.wait_ge(s_add, n - 1)
                        sp.dma_start(work[:, (n % 2) * PW:(n % 2 + 1) * PW], s_[:, i * PW:(i + 1) * PW]).then_inc(s_tl[n % 2], 16)
                    if L == 1:
                        sp.wait_ge(s_piece, i + 1)
                        o = work[:, (2 + i % 2) * PW:(3 + i % 2) * PW]
                        a, b = i * PW, (i + 1) * PW
                        full = N // HI
                        tail = (N - full * HI) * D
                        ov = out.rearrange("n d -> (n d)")
                        main = ov[0:full * HI * D].rearrange("(p f) -> p f", f=HI * D)
                        cut = full // 16 * 16
                        sp.dma_start(main[0:cut, a:b], o[0:cut, :]).then_inc(s_outd[i % 2], 16)
                        sp.dma_start(main[cut:full, a:b], o[cut:full, :]).then_inc(s_outd[i % 2], 16)
                        w = min(b, tail) - a
                        if w > 0:
                            sp.dma_start(ov[full * HI * D + a:full * HI * D + a + w].rearrange("(o f) -> o f", o=1), o[full:full + 1, 0:w]).then_inc(s_outd[i % 2], 16)
            for i in (PIECES - 2, PIECES - 1):
                sp.wait_ge(s_outd[i % 2], stored(i))

        @block.gpsimd
        def _(pool):
            pool.iota(iota[:, :], [[1, HI]], base=0, channel_multiplier=0, allow_small_or_imprecise_dtypes=True).then_inc(s_const, 1)
            pool.iota(pid[:, :], [[0, 1]], base=0, channel_multiplier=1, allow_small_or_imprecise_dtypes=True).then_inc(s_const, 1)
            pool.iota(trash[:, :], [[0, 1]], base=NP, channel_multiplier=1, allow_small_or_imprecise_dtypes=True).then_inc(s_const, 1)
            pool.memset(ident[:, :], 0.0).then_inc(s_const, 1)
            pool.memset(earlier[:, :], 1.0).then_inc(s_const, 1)
            pool.memset(zero[:, :], 0.0).then_inc(s_const, 1)
            pool.memset(eps[:, 0:1], EPS_LN).then_inc(s_const, 1)
            pool.memset(eps[:, 1:2], EPS_DEG).then_inc(s_const, 1)
            pool.wait_ge(s_const, 8)
            pool.affine_select(out=ident[:, :], in_=ident[:, :], compare_op=ALU.not_equal, fill=1.0, base=0,
                               pattern=[[-1, P]], channel_multiplier=1).then_inc(s_const, 1)
            pool.affine_select(out=earlier[:, :], in_=earlier[:, :], compare_op=ALU.is_gt, fill=0.0, base=0,
                               pattern=[[-1, P]], channel_multiplier=1).then_inc(s_const, 1)
            pool.wait_ge(s_span, 2)
            pool.partition_all_reduce(wide[:, 1:2], wide[:, 0:1], P, bass.bass_isa.ReduceOp.max).then_inc(s_wide, 1)
            pool.wait_ge(s_local, 1)
            is_local = pool.value_load(local[0:1, 0:1], min_val=0, max_val=1)
            for L in range(2):
                base = L * NS
                pool.wait_ge(s_yd, 16 * (L + 1))
                pool.wait_ge(s_zero[L], 16 * CH * 8)

                def add_messages(i, h):
                    t = i * 2 + h
                    pool.wait_ge(s_mo, base + t + 1)
                    for k in range(CH):
                        wait(pool, s_tab[k], (base + t) * 16)
                        pool.nop(nofuse=True)
                        pool.indirect_dma_start(
                            out=tab_d[L][k], out_offset=bass.IndirectOffsetOnAxis(ap=ridx[:, h, k:k + 1], axis=0),
                            in_=Mo[:, h, k, :], in_offset=None, compute_op=ALU.add).then_inc(s_tab[k], 16)

                def body_local(i):
                    for h in range(2):
                        pool.wait_ge(s_idx, base + i * 2 + h + 1)
                        add_messages(i, h)

                def body(i):
                    for h in range(2):
                        t = i * 2 + h
                        pool.wait_ge(s_idx, base + t + 1)
                        wait(pool, s_pm, base + t - 1)
                        pool.nop(nofuse=True)
                        for k in range(CH):
                            pool.indirect_dma_start(
                                out=G[:, h, k, :], out_offset=None, in_=y_d[L],
                                in_offset=bass.IndirectOffsetOnAxis(ap=cidx[:, h, k:k + 1], axis=0)).then_inc(s_gat[h], 16)
                        add_messages(i, h)
                with pool.If(is_local):
                    steps(pool, NS // 2, body_local)
                with pool.Else():
                    steps(pool, NS // 2, body)
            for k in range(CH):
                pool.wait_ge(s_tab[k], 16 * NS * 2)

        @block.scalar
        def _(act):
            def clear_tables(L):
                for k in range(CH):
                    t = tab_d[L][k].rearrange("(p r) d -> p (r d)", p=P)
                    for i in range(8):
                        act.dma_start(t[:, i * ZW:(i + 1) * ZW], zero[:, :]).then_inc(s_zero[L], 16)
            act.wait_ge(s_const, 8)
            clear_tables(0)
            act.wait_ge(s_v2a, 1)
            act.activation(logit[:, :], ga[:, :], ACT.Ln).then_inc(s_a2v, 1)
            act.activation(gb[:, :], ga[:, :], ACT.Ln, bias=1.0, scale=-1.0).then_inc(s_a2v, 1)
            for p_ in range(PIECES):
                act.wait_ge(s_v2a, 2 + p_)
                act.activation(st[:, 1, :], st[:, 0, :], ACT.Sqrt, bias=eps[:, 0:1], scale=1.0 / D).then_inc(s_a2v, 1)
            act.wait_ge(s_w, 16 * 14)
            act.wait_ge(s_local, 1)
            is_local = act.value_load(local[0:1, 0:1], min_val=0, max_val=1)
            for L in range(2):
                base = L * NS

                def node_group(g, slot):
                    n = L * NG + g
                    hT = Z[0:D, slot * 384:(slot + 1) * 384]
                    rT = Z[:, 768 + slot * 384:768 + (slot + 1) * 384]
                    act.wait_ge(s_T, n + 1)
                    act.activation(hT, psG[0:D, slot, 0:384], ACT.Copy).then_inc(s_hT, 1)
                    act.wait_ge(s_mm, n + 1)
                    wait(act, s_sm, n - 1)
                    act.activation(rT, psG[:, 2 + slot, 0:384], ACT.Relu, bias=bias[L][:, 0:1]).then_inc(s_rT, 1)

                def pair(i):
                    for s in range(2):
                        node_group(i * 2 + s, s)
                steps(act, NG // 2, pair)
                node_group(NG - 1, 0)

                def col_values(i):
                    for h in range(2):
                        t = i * 2 + h
                        act.wait_ge(s_g[1], base + t + 1)
                        act.activation(gb[:, bass.ds(t * CH, CH)], psR[:, h, 0:CH], ACT.Copy).then_inc(s_sel[1], 1)
                with act.If(is_local):
                    steps(act, NS // 2, col_values)
                with act.Else():
                    act.nop()
                act.wait_ge(s_v2a, 2 + PIECES + 2 * L)
                act.activation(gb[:, :], ga[:, :], ACT.Sigmoid).then_inc(s_a2v, 1)
                act.wait_ge(s_mask, L + 1)

                def weigh(i):
                    for h in range(2):
                        t = i * 2 + h
                        act.wait_ge(s_oab, base + t + 1)
                        wait(act, s_acm, base + t - 1)
                        for k in range(CH):
                            act.activation(OAw[L][:, h, k, :], OA[L][:, h, k, :], ACT.Copy,
                                           scale=ga[:, bass.ds(t * CH + k, 1)]).then_inc(s_oaw, 1)
                steps(act, NS // 2, weigh)
                act.wait_ge(s_v2a, 3 + PIECES + 2 * L)
                act.activation(dinv[:, :], abr[:, 0, :], ACT.Sqrt).then_inc(s_a2v, 1)
                if L == 0:
                    clear_tables(1)

                def messages(i, h):
                    t = i * 2 + h
                    act.wait_ge(s_pm, base + t + 1)
                    for k in range(CH):
                        wait(act, s_tab[k], (base + t - 1) * 16)
                    act.activation(Mo[:, h, :, :].rearrange("p k d -> p (k d)"), psG[:, h, :], ACT.Copy).then_inc(s_mo, 1)

                def body(i):
                    for h in range(2):
                        messages(i, h)

                def body_local(i):
                    for h in range(2):
                        act.wait_ge(s_ge, base + i * 2 + h + 1)
                        wait(act, s_pm, base + i * 2 + h - 1)
                        act.activation(G[:, h, :, :].rearrange("p k d -> p (k d)"), psG[:, 2 + h, :], ACT.Copy).then_inc(s_gev, 1)
                        messages(i, h)
                with act.If(is_local):
                    steps(act, NS // 2, body_local)
                with act.Else():
                    steps(act, NS // 2, body)

        @block.vector
        def _(dve):
            chained = [0]

            def link(ins):
                chained[0] += 1
                ins.then_inc(s_dve, 1)
                dve.wait_ge(s_dve, chained[0])

            dve.memset(A[0].bitcast(i32), PAD_ROW).then_inc(s_pad, 1)
            dve.memset(A[1].bitcast(i32), N - 1).then_inc(s_pad, 1)
            dve.memset(A[2], 0.5).then_inc(s_pad, 1)
            dve.memset(att[0][:, :], 0.0)
            dve.memset(att[1][:, :], 0.0).then_inc(s_pad, 1)

            def split(a, q, r):
                link(dve.tensor_scalar(q.bitcast(i32), a, 1.0 / HI, None, ALU.mult))
                link(dve.tensor_copy(q, q.bitcast(i32)))
                link(dve.scalar_tensor_tensor(r, q, -float(HI), a, ALU.mult, ALU.add))
                link(dve.scalar_tensor_tensor(q, r, 0.0, q, ALU.is_lt, ALU.subtract))
                link(dve.scalar_tensor_tensor(q, r, float(HI), q, ALU.is_ge, ALU.subtract))
                link(dve.scalar_tensor_tensor(a, q, -float(HI), a, ALU.mult, ALU.add))

            dve.wait_ge(s_row, 48)
            link(dve.tensor_copy(A[0], A[0].bitcast(i32)))
            dve.tensor_copy(U[0], A[0]).then_inc(s_u16, 1)
            split(A[0], B[0], B[2])
            dve.tensor_copy(U[1], B[0]).then_inc(s_u16, 1)
            dve.wait_ge(s_col, 48)
            link(dve.tensor_copy(A[1], A[1].bitcast(i32)))
            cols = A[1].rearrange("p (j e) -> p j e", j=RJ)
            link(dve.memset(wide[:, :], 0.0))
            link(dve.tensor_reduce(span[0:RP, 0, :], cols, AX.X, ALU.min))
            link(dve.tensor_scalar(span[0:RP, 0, :], span[0:RP, 0, :], float(NP - P), None, ALU.min))
            link(dve.tensor_reduce(span[0:RP, 1, :], cols, AX.X, ALU.max))
            link(dve.tensor_tensor(span[0:RP, 1, :], span[0:RP, 1, :], span[0:RP, 0, :], ALU.subtract))
            dve.tensor_copy(span[0:RP, 2, :].bitcast(i32), span[0:RP, 0, :]).then_inc(s_span, 1)
            dve.tensor_reduce(wide[0:RP, 0:1], span[0:RP, 1, :], AX.X, ALU.max).then_inc(s_span, 1)
            dve.tensor_tensor(U[3].rearrange("p (j e) -> p j e", j=RJ), cols, span[0:RP, 0, :].unsqueeze(2).to_broadcast([RP, RJ, SE]), ALU.subtract).then_inc(s_u16, 1)
            dve.wait_ge(s_u16, 3)
            split(A[1], B[1], B[2])
            dve.tensor_copy(U[2], B[1]).then_inc(s_u16, 1)
            dve.wait_ge(s_nz, 48)
            dve.tensor_copy(B[2][:, 0:1], B[2][:, 0:1]).then_inc(s_split, 1)
            dest = [lof, hif, rowf, chif, gb]
            n = 0
            for a, d in enumerate(dest):
                dv = d[:, :].rearrange("q (p j k) -> q j k p", j=RJ, k=CH)
                for j in range(RJ):
                    for kk in range(2):
                        dve.wait_ge(s_tp, n + 1)
                        if a == 2 and j == 0 and kk == 0:
                            dve.wait_ge(s_scr, 64)
                        dve.tensor_copy(dv[:, j, 4 * kk:4 * kk + 4, :],
                                        psG[:, n % 6, 0:4 * RP].rearrange("q (k p) -> q k p", k=4)).then_inc(s_tpe, 1)
                        n += 1
            dve.wait_ge(s_tpe, n)
            link(dve.scalar_tensor_tensor(coli[:, :], rowf[:, :], float(HI), chif[:, :], ALU.mult, ALU.add))
            link(dve.scalar_tensor_tensor(rowf[:, :], lof[:, :], float(HI), hif[:, :], ALU.mult, ALU.add))
            dve.tensor_scalar(ga[:, :], gb[:, :], EPS_NOISE, 1.0 - EPS_NOISE, ALU.max, ALU.min).then_inc(s_v2a, 1)
            dve.wait_ge(s_a2v, 2)
            link(dve.tensor_tensor(logit[:, :], logit[:, :], gb[:, :], ALU.subtract))
            dve.wait_ge(s_wide, 1)
            dve.tensor_scalar(local[:, :], wide[:, 1:2], float(P - 1), None, ALU.is_le).then_inc(s_local, 1)
            dve.wait_ge(s_local, 1)
            is_local = dve.value_load(local[0:1, 0:1], min_val=0, max_val=1)
            link(dve.memset(cur[96:P, :], 0.0))
            dve.sem_inc(s_split, 3)
            dve.wait_ge(s_x, 48)
            dve.wait_ge(s_const, 10)
            for p_ in range(PIECES):
                def piece(t):
                    return t[:, p_ * PW:(p_ + 1) * PW].rearrange("p (h d) -> p h d", d=D)
                sq = Z[:, 0:PW].rearrange("p (h d) -> p h d", d=D)
                s0, s1 = st[:, 0, :], st[:, 1, :]
                link(dve.tensor_reduce(s0, piece(cur), AX.X, ALU.add))
                link(dve.tensor_scalar(s1, s0, 1.0 / D, None, ALU.mult))
                link(dve.tensor_tensor(piece(work), piece(cur), s1.unsqueeze(2).to_broadcast([P, PH, D]), ALU.subtract))
                link(dve.tensor_tensor(sq, piece(work), piece(work), ALU.mult))
                dve.tensor_reduce(s0, sq, AX.X, ALU.add).then_inc(s_v2a, 1)
                dve.wait_ge(s_a2v, 3 + p_)
                link(dve.reciprocal(s0, s1))
                link(dve.tensor_tensor(piece(work), piece(work), s0.unsqueeze(2).to_broadcast([P, PH, D]), ALU.mult))
                link(dve.tensor_scalar(piece(work), piece(work), 0.0, None, ALU.max))
                link(dve.tensor_tensor(piece(cur), piece(cur), piece(work), ALU.add))
            dve.sem_inc(s_acc, 1)

            for L in range(2):
                base = L * NS

                def stage(g, slot):
                    wait(dve, s_T, L * NG + g - 1)
                    dve.tensor_copy(Xs[:, slot, :], X[L][:, bass.ds(g * (GH * D), GH * D)]).then_inc(s_stg, 1)

                def node_group(g, slot):
                    n = L * NG + g
                    dve.wait_ge(s_sm, n + 1)
                    dve.tensor_copy(ab[:, bass.ds(g * GH, GH), :], psG[:, 4 + slot, 0:2 * GH].rearrange("p (h t) -> p h t", t=2)).then_inc(s_ab, 1)

                def pair(i):
                    for s in range(2):
                        stage(i * 2 + s, s)
                    for s in range(2):
                        node_group(i * 2 + s, s)
                steps(dve, NG // 2, pair)
                stage(NG - 1, 0)
                node_group(NG - 1, 0)
                dve.wait_ge(s_ab, NG * (L + 1))
                dve.tensor_copy(bt[:, :], ab[:, :, 1]).then_inc(s_bt, 1)
                abv = ab[:, :, :].rearrange("p h t -> p t h")
                link(dve.tensor_copy(abs3[:, 0, :, :], abv))
                link(dve.tensor_tensor(abr[:, :, :], abv, abs3[:, 0, :, :], ALU.subtract))
                link(dve.tensor_copy(abs3[:, 1, :, :], abr[:, :, :]))
                link(dve.tensor_tensor(abr[:, :, :], abr[:, :, :], abs3[:, 1, :, :], ALU.subtract))
                dve.tensor_copy(abs3[:, 2, :, :], abr[:, :, :]).then_inc(s_abs, 1)

                def one_hot(t, i):
                    dve.wait_ge(s_lo[t], (base + i + 1) * 16)
                    wait(dve, s_g[t], base + i)
                    dve.tensor_scalar(ones_lo[:, t, :], lo_bc[:, t, :], pid[:, 0:1], None, ALU.is_equal).then_inc(s_oh[t], 1)

                def select(t, i):
                    dve.wait_ge(s_g[t], base + i + 1)
                    wait(dve, s_sel[t], base + i)
                    for k in range(CH):
                        c = i * CH + k
                        ins = dve.scalar_tensor_tensor(
                            junk[t][:, k, :], iota[:, :], (hif, chif)[t][:, bass.ds(c, 1)],
                            psG[:, 3 * t + k // 3, (k % 3) * HI:(k % 3 + 1) * HI], ALU.is_equal, ALU.mult,
                            accum_out=(ga, gb)[t][:, bass.ds(c, 1)])
                    ins.then_inc(s_sel[t], 1)

                def gather(i, last=False):
                    one_hot(1, i)
                    select(0, i)
                    if not last:
                        one_hot(0, i + 1)
                    select(1, i)

                def row_one_hot(i, h):
                    dve.wait_ge(s_rl[h], (base // 2 + i + 1) * 16)
                    wait(dve, s_g[0], base + i * 2 + h - 1)
                    dve.tensor_scalar(ones_lo[:, h, :], lo_bc[:, h, :], pid[:, 0:1], None, ALU.is_equal).then_inc(s_oh[0], 1)

                def gather_local(i, last=False):
                    for h in range(2):
                        t = i * 2 + h
                        if not (last and h == 1):
                            row_one_hot(i + h, 1 - h)
                        dve.wait_ge(s_cb[h], (base // 2 + i + 1) * 16)
                        wait(dve, s_g[1], base + t - 1)
                        dve.tensor_scalar(OC[:, h, :], row_bc[:, h, :], pid[:, 0:1], None, ALU.is_equal).then_inc(s_oh[1], 1)
                        dve.wait_ge(s_g[0], base + t + 1)
                        wait(dve, s_sel[0], base + t)
                        for k in range(CH):
                            c = t * CH + k
                            ins = dve.scalar_tensor_tensor(
                                junk[0][:, k, :], iota[:, :], hif[:, bass.ds(c, 1)],
                                psG[:, 3 * h + k // 3, (k % 3) * HI:(k % 3 + 1) * HI], ALU.is_equal, ALU.mult,
                                accum_out=ga[:, bass.ds(c, 1)])
                        ins.then_inc(s_sel[0], 1)
                with dve.If(is_local):
                    row_one_hot(0, 0)
                    gather_local(0)
                    with dve.Fori(1, NS // 2 - 1) as i:
                        gather_local(i)
                    gather_local(NS // 2 - 1, True)
                with dve.Else():
                    one_hot(0, 0)
                    with dve.Fori(0, NS - 1) as i:
                        gather(i)
                    gather(NS - 1, True)
                dve.wait_ge(s_sel[0], base + NS)
                dve.wait_ge(s_sel[1], base + NS)
                link(dve.scalar_tensor_tensor(ga[:, :], ga[:, :], attb[L][:, 0:1], gb[:, :], ALU.add, ALU.add))
                dve.tensor_tensor(ga[:, :], ga[:, :], logit[:, :], ALU.add).then_inc(s_v2a, 1)
                dve.wait_ge(s_a2v, 3 + PIECES + 2 * L)
                link(dve.tensor_scalar(ga[:, :], gb[:, :], ZETA - GAMMA, GAMMA, ALU.mult, ALU.add))
                dve.tensor_scalar(ga[:, :], ga[:, :], 0.0, 1.0, ALU.max, ALU.min).then_inc(s_mask, 1)
                dve.wait_ge(s_mask, L + 1)
                if L == 0:
                    dve.wait_ge(s_accd, 16)

                def scatter(i):
                    for h in range(2):
                        t = i * 2 + h
                        wait(dve, s_acm, base + t - 1)
                        dve.tensor_tensor(OA[L][:, h, :, :], iota[:, 0:P].unsqueeze(1).to_broadcast([P, CH, P]),
                                          lof[:, bass.ds(t * CH, CH)].unsqueeze(2).to_broadcast([P, CH, P]), ALU.is_equal).then_inc(s_oab, 1)
                        dve.tensor_tensor(OB[L][:, h, :, :], iota[:, :].unsqueeze(1).to_broadcast([P, CH, HI]),
                                          hif[:, bass.ds(t * CH, CH)].unsqueeze(2).to_broadcast([P, CH, HI]), ALU.is_equal).then_inc(s_ob, 1)
                steps(dve, NS // 2, scatter)
                dve.wait_ge(s_R, L + 1)
                dve.tensor_scalar(abr[:, 0, :], psR[:, 0, 0:HI], EPS_DEG, None, ALU.add).then_inc(s_v2a, 1)
                dve.wait_ge(s_a2v, 4 + PIECES + 2 * L)
                link(dve.reciprocal(abr[:, 1, :], dinv[:, :]))
                link(dve.tensor_scalar(dinv[:, :], abr[:, 1, :], 0.0, 10.0, ALU.max, ALU.min))
                dve.tensor_tensor(Y[L][:, :].rearrange("p (h d) -> p h d", d=D), X[L][:, :].rearrange("p (h d) -> p h d", d=D),
                                  dinv[:, :].unsqueeze(2).to_broadcast([P, HI, D]), ALU.mult).then_inc(s_y, 1)

                def body(i, by_window):
                    for h in range(2):
                        t = i * 2 + h
                        c = t * CH
                        wait(dve, s_idx, base + t)
                        dve.wait_ge(s_rb[h], ((base // 2) + i + 1) * 16)
                        for k in range(CH):
                            dve.scalar_tensor_tensor(junk2[:, k, :], row_bc[:, h, k * P:(k + 1) * P], rowf[:, bass.ds(c + k, 1)],
                                                     earlier[:, :], ALU.is_equal, ALU.mult, accum_out=cnt[:, k:k + 1])
                        for k in range(CH):
                            wait(dve, s_tab[k], (base + t - 1) * 16)
                        dve.tensor_copy(cidx[:, h, :], coli[:, bass.ds(c, CH)])
                        dve.tensor_scalar(dtmp[:, :], rowf[:, bass.ds(c, CH)], -1.0, trash[:, 0:1], ALU.mult, ALU.add).then_inc(s_cnt, 1)
                        dve.wait_ge(s_cnt, (base + t) * 2 + 1)
                        dve.scalar_tensor_tensor(dtmp[:, :], cnt[:, :], 1.0, dtmp[:, :], ALU.min, ALU.mult).then_inc(s_cnt, 1)
                        dve.wait_ge(s_cnt, (base + t) * 2 + 2)
                        dve.tensor_tensor(ridx[:, h, :], dtmp[:, :], rowf[:, bass.ds(c, CH)], ALU.add).then_inc(s_idx, 1)
                        if by_window:
                            dve.wait_ge(s_cb2[h], (base // 2 + i + 1) * 16)
                            wait(dve, s_ge, base + t - 1)
                            dve.tensor_scalar(OC[:, h, :], lo_bc[:, h, :], pid[:, 0:1], None, ALU.is_equal).then_inc(s_oc, 1)
                        wait(dve, s_pm, base + t - 1)
                        for k in range(CH):
                            ins = dve.tensor_scalar(Sw[:, h, k, :], row_bc[:, h, k * P:(k + 1) * P], rowf[:, bass.ds(c + k, 1)],
                                                    ga[:, bass.ds(c + k, 1)], ALU.is_equal, ALU.mult)
                        ins.then_inc(s_sw, 1)
                with dve.If(is_local):
                    steps(dve, NS // 2, lambda i: body(i, True))
                with dve.Else():
                    steps(dve, NS // 2, lambda i: body(i, False))

                parts = CH + L
                before = 0 if L == 0 else PIECES * CH
                for p_ in range(PIECES):
                    S = work[:, (2 + p_ % 2) * PW:(3 + p_ % 2) * PW]
                    if L == 1 and p_ >= 2:
                        dve.wait_ge(s_outd[p_ % 2], stored(p_ - 2))
                    for k in range(parts):
                        n = before + p_ * parts + k
                        dve.wait_ge(s_tl[n % 2], 16 * (n // 2 + 1))
                        T = work[:, (n % 2) * PW:(n % 2 + 1) * PW]
                        if k == 0:
                            ins = dve.tensor_copy(S, T)
                        else:
                            ins = dve.tensor_tensor(S, S, T, ALU.add)
                        ins.then_inc(s_add, 1)
                        dve.wait_ge(s_add, n + 1)
                        if k == CH - 1:
                            Sv = S.rearrange("p (h d) -> p h d", d=D)
                            dv = dinv[:, p_ * PH:(p_ + 1) * PH].unsqueeze(2).to_broadcast([P, PH, D])
                            C = cur[:, p_ * PW:(p_ + 1) * PW]
                            if L == 0:
                                link(dve.tensor_tensor(C.rearrange("p (h d) -> p h d", d=D), Sv, dv, ALU.mult))
                            else:
                                link(dve.tensor_tensor(Sv, Sv, dv, ALU.mult))
                                link(dve.tensor_tensor(S, S, C, ALU.add))
                    if L == 1:
                        dve.sem_inc(s_piece, 1)

        @block.tensor
        def _(pe):
            pe.wait_ge(s_const, 10)
            n = 0
            pe.wait_ge(s_split, 1)
            for a in (B[0], A[0], B[1], A[1], A[2]):
                for j in range(RJ):
                    for kk in range(2):
                        if n >= 6:
                            pe.wait_ge(s_tpe, n - 5)
                        for k in range(4):
                            f = (j * CH + kk * 4 + k) * P
                            ins = pe.transpose(psG[:, n % 6, k * RP:(k + 1) * RP], a[:, f:f + P], ident[0:RP, 0:RP])
                        ins.then_inc(s_tp, 1)
                        n += 1
            pe.wait_ge(s_w, 16 * 14)
            pe.wait_ge(s_local, 1)
            is_local = pe.value_load(local[0:1, 0:1], min_val=0, max_val=1)
            for L in range(2):
                base = L * NS

                def pair(i, slots=2):
                    for s in range(slots):
                        g = i * 2 + s
                        pe.wait_ge(s_stg, L * NG + g + 1)
                        pe.nop(nofuse=True)
                        for b in range(GH):
                            ins = pe.transpose(psG[0:D, s, b * P:(b + 1) * P], Xs[:, s, b * D:(b + 1) * D], ident[:, :])
                        ins.then_inc(s_T, 1)
                    for s in range(slots):
                        n = L * NG + i * 2 + s
                        pe.wait_ge(s_hT, n + 1)
                        wait(pe, s_rT, n - 1)
                        pe.matmul(psG[:, 2 + s, 0:384], W[L][:, :], Z[0:D, s * 384:(s + 1) * 384], start=True, stop=True).then_inc(s_mm, 1)
                    for s in range(slots):
                        n = L * NG + i * 2 + s
                        pe.wait_ge(s_rT, n + 1)
                        wait(pe, s_ab, n - 1)
                        rT = Z[:, 768 + s * 384:768 + (s + 1) * 384]
                        for b in range(GH):
                            ins = pe.matmul(psG[:, 4 + s, 2 * b:2 * b + 2], rT[:, b * P:(b + 1) * P], att[L][:, :], start=True, stop=True)
                        ins.then_inc(s_sm, 1)
                steps(pe, NG // 2, pair)
                pair(NG // 2, 1)

                pe.wait_ge(s_abs, L + 1)

                def gather(i):
                    for t in range(2):
                        pe.wait_ge(s_oh[t], base + i + 1)
                        wait(pe, s_sel[t], base + i)
                        for k in range(CH):
                            for m in range(3):
                                ins = pe.matmul(psG[:, 3 * t + k // 3, (k % 3) * HI:(k % 3 + 1) * HI],
                                                ones_lo[:, t, k * P:(k + 1) * P], abs3[:, m, t, :], start=m == 0, stop=m == 2)
                        ins.then_inc(s_g[t], 1)

                def gather_local(i):
                    for h in range(2):
                        t = i * 2 + h
                        pe.wait_ge(s_oh[0], base + t + 1)
                        wait(pe, s_sel[0], base + t - 1)
                        for k in range(CH):
                            for m in range(3):
                                ins = pe.matmul(psG[:, 3 * h + k // 3, (k % 3) * HI:(k % 3 + 1) * HI],
                                                ones_lo[:, h, k * P:(k + 1) * P], abs3[:, m, 0, :], start=m == 0, stop=m == 2)
                        ins.then_inc(s_g[0], 1)
                        pe.wait_ge(s_oh[1], base + t + 1)
                        pe.wait_ge(s_bw[h], (base // 2 + i + 1) * 16)
                        wait(pe, s_sel[1], base + t - 1)
                        for k in range(CH):
                            ins = pe.matmul(psR[:, h, k:k + 1], OC[:, h, k * P:(k + 1) * P], bw[:, h:h + 1], start=True, stop=True)
                        ins.then_inc(s_g[1], 1)
                with pe.If(is_local):
                    steps(pe, NS // 2, gather_local)
                with pe.Else():
                    steps(pe, NS, gather)

                pe.wait_ge(s_sel[1], base + NS)
                pe.matmul(psR[:, 0, 0:HI], zero[:, 0:P], zero[:, 0:HI], start=True, stop=False)

                def scatter(i):
                    for h in range(2):
                        t = i * 2 + h
                        pe.wait_ge(s_ob, base + t + 1)
                        for k in range(CH):
                            pe.wait_ge(s_oaw, (base + t) * CH + k + 1)
                            ins = pe.matmul(psR[:, 0, 0:HI], OAw[L][:, h, k, :], OB[L][:, h, k, :], start=False, stop=False)
                        ins.then_inc(s_acm, 1)
                steps(pe, NS // 2, scatter)
                pe.matmul(psR[:, 0, 0:HI], zero[:, 0:P], zero[:, 0:HI], start=False, stop=True).then_inc(s_R, 1)

                def body(i, by_window):
                    for h in range(2):
                        t = i * 2 + h
                        if by_window:
                            pe.wait_ge(s_oc, base + t + 1)
                            pe.wait_ge(s_yw[h], (base // 2 + i + 1) * 16)
                            wait(pe, s_gev, base + t - 1)
                            for k in range(CH):
                                ins = pe.matmul(psG[:, 2 + h, k * D:(k + 1) * D], OC[:, h, k * P:(k + 1) * P], yw[:, h, :], start=True, stop=True)
                            ins.then_inc(s_ge, 1)
                            pe.wait_ge(s_gev, base + t + 1)
                        else:
                            pe.wait_ge(s_gat[h], (base // 2 + i + 1) * 16 * CH)
                        pe.wait_ge(s_sw, base + t + 1)
                        wait(pe, s_mo, base + t - 1)
                        for k in range(CH):
                            ins = pe.matmul(psG[:, h, k * D:(k + 1) * D], Sw[:, h, k, :], G[:, h, k, :], start=True, stop=True)
                        ins.then_inc(s_pm, 1)
                with pe.If(is_local):
                    steps(pe, NS // 2, lambda i: body(i, True))
                with pe.Else():
                    steps(pe, NS // 2, lambda i: body(i, False))


_PARAMS = ['nbW', 'nbb', 'selfW', 'selfb', 'attW', 'attb']
_INS = ['x', 'src', 'dst', 'edge_weight1'] + [f'L0_gnn_{p}{L}' for L in range(2) for p in _PARAMS]


def kernel(**inputs):
    import numpy as _np
    import concourse.bacc as _bacc
    from concourse import mybir as _mybir
    from concourse.bass_utils import run_bass_kernel_spmd as _run
    nc = _bacc.Bacc("TRN2", target_bir_lowering=False, num_devices=1)
    arrays, args = {}, []
    for name in _INS:
        a = _np.ascontiguousarray(inputs[name])
        arrays[f"in_{name}_dram"] = a
        args.append(nc.dram_tensor(f"in_{name}_dram", a.shape, _mybir.dt.from_np(a.dtype), kind="ExternalInput").ap())
    out = nc.dram_tensor("out_0_dram", (N, D), _mybir.dt.float32, kind="ExternalOutput").ap()
    build(nc, *args[:4], [args[4:10], args[10:16]], out)
    r = _run(nc, [arrays], core_ids=[0])
    return r.results[0]["out_0_dram"]
```

```python
import concourse.bass as bass
from concourse import mybir
from contextlib import ExitStack

N, D, E = 18750, 64, 318750
P = 128
HI = -(-N // P)
NP = P * HI
CH = 8
SE = CH * P
RJ = 3
RP = -(-E // (SE * RJ))
NS = RP * RJ
NB = 144
NA = NS - NB
FAR = 6
NLAST = 30
NC = NS * CH
RW = RJ * SE
PARTS = ((0, NA), (NA, NS - NLAST), (NS - NLAST, NS))
EP = NS * SE
PAD_ROW = NP
TABLE_ROWS = NP + P
GAMMA, ZETA = -0.45, 1.05
EPS_NOISE, EPS_DEG, EPS_LN = 1e-7, 1e-6, 1e-5
PIECES = 7
PH = HI // PIECES
PW = PH * D
YP = 3
YW = HI // YP * D
ZW = TABLE_ROWS * D // P // 8
GH = 3
NG = HI // GH
GP = PH // GH
assert HI % PIECES == 0 and PH % GH == 0 and GP % 2 == 1 and NA % FAR == 0 and NB % FAR == 0 and NA % 2 == 0 and NLAST % 2 == 0


def build(nc, x, src, dst, noise, params, out):
    f32, bf16, i32, u16 = mybir.dt.float32, mybir.dt.bfloat16, mybir.dt.int32, mybir.dt.uint16
    ALU, ACT, AX = mybir.AluOpType, mybir.ActivationFunctionType, mybir.AxisListType

    row_d = nc.dram_tensor("row_d", (EP,), u16).ap()
    rlo_d = nc.dram_tensor("rlo_d", (EP,), u16).ap()
    crel_d = nc.dram_tensor("crel_d", (EP,), u16).ap()
    a_d = [nc.dram_tensor(f"a_d{L}", (NP + 1, 1), f32).ap() for L in range(2)]
    base_d = nc.dram_tensor("base_d", (NS,), i32).ap()
    b_d = [nc.dram_tensor(f"b_d{L}", (NP, 3), bf16).ap() for L in range(2)]
    clo_d = nc.dram_tensor("clo_d", (EP,), u16).ap()
    acc_d = nc.dram_tensor("acc_d", (P, HI * D), f32).ap()
    y_d = [nc.dram_tensor(f"y_d{L}", (NP, D), f32).ap() for L in range(2)]
    tab_d = [[nc.dram_tensor(f"tab_d{L}_{k}", (TABLE_ROWS, D), f32).ap() for k in range(CH)] for L in range(2)]

    ctx = ExitStack()
    with ctx:
        def sb(name, shape, dt):
            return ctx.enter_context(nc.sbuf_tensor(name, shape, dt))

        def sem(name):
            return ctx.enter_context(nc.semaphore(name))

        cur = sb("cur", [P, HI * D], f32)
        work = sb("work", [P, HI * D], f32)
        rowf = sb("rowf", [P, NC], f32)
        lof = sb("lof", [P, NC], bf16)
        hif = sb("hif", [P, NC], f32)
        chif = sb("chif", [P, NC], f32)
        coli = sb("coli", [P, NC], i32)
        logit = sb("logit", [P, NC], f32)
        ga = sb("ga", [P, NC], f32)
        gb = sb("gb", [P, NC], f32)
        ones_lo = sb("ones_lo", [P, 2, SE], bf16)
        lo_bc = sb("lo_bc", [P, 2, SE], u16)
        row_bc = sb("row_bc", [P, 2, SE], u16)
        scratch = sb("scratch", [P, CH * (P + HI)], f32)
        y_edge = sb("y_edge", [P, 2, CH, D], f32)
        merge = sb("merge", [P, 2, CH, P], f32)
        msg = work[:, 0:4 * CH * D].rearrange("p (u k d) -> p u k d", u=4, k=CH)
        zero = sb("zero", [P, ZW], f32)
        iota = sb("iota", [P, HI], f32)
        pid = sb("pid", [P, 1], f32)
        trash = sb("trash", [P, 1], f32)
        ident = sb("ident", [P, P], f32)
        earlier = sb("earlier", [P, P], f32)
        W = [sb(f"W{L}", [D, 2 * D], f32) for L in range(2)]
        bias = [sb(f"bias{L}", [P, 1], f32) for L in range(2)]
        att = [sb(f"att{L}", [P, 2], f32) for L in range(2)]
        attb = [sb(f"attb{L}", [P, 1], f32) for L in range(2)]
        ab = sb("ab", [P, HI, 2], f32)
        ab_parts = sb("ab_parts", [P, 3, 2, HI], bf16)
        abr = sb("abr", [P, 2, HI], f32)
        a_out = sb("a_out", [P, HI], f32)
        iota8 = sb("iota8", [P, P, CH], bf16)
        aidx = sb("aidx", [P, 2, CH], i32)
        arow = sb("arow", [P, 2, CH], f32)
        npid = sb("npid", [P, 1], f32)
        st = sb("st", [P, 2, PH], f32)
        eps = sb("eps", [P, 2], f32)
        dinv = sb("dinv", [P, HI], f32)
        ridx = sb("ridx", [P, 4, CH], i32)
        cidx = sb("cidx", [P, 2, CH], i32)
        cnt = sb("cnt", [P, CH], f32)
        dtmp = sb("dtmp", [P, CH], f32)
        psG = ctx.enter_context(nc.psum_tensor("psG", [P, 6, 512], f32))
        psR = ctx.enter_context(nc.psum_tensor("psR", [P, 2, 512], f32))
        b_out = sb("b_out", [P, HI, 3], bf16)
        b_window = sb("b_window", [P, FAR, 4], bf16)
        y_window = sb("y_window", [P, 2, D], f32)
        bases = sb("bases", [1, NS], i32)
        span = sb("span", [P, 3, RJ], f32)
        wide = sb("wide", [P, 2], f32)
        local = sb("local", [P, 1], i32)
        window_one_hot = scratch[:, 0:SE].bitcast(bf16).rearrange("p (h n) -> p h n", h=2)
        dist = scratch[:, SE:SE + SE // 2].bitcast(bf16)
        window_one_hot_f32 = scratch[:, 0:2 * SE].rearrange("p (h n) -> p h n", h=2)
        junk = [t.rearrange("p (k n) -> p k n", k=CH) for t in
                (merge[:, :, :, :].rearrange("p a k n -> p (a k n)")[:, 0:CH * HI], scratch[:, 0:CH * HI])]
        same = ones_lo[:, :, :].rearrange("p h e -> p (h e)").bitcast(f32).rearrange("p (k n) -> p k n", k=CH)
        x_staged = scratch[:, 1536:1536 + 2 * GH * D].rearrange("p (s n) -> p s n", s=2)
        hT = [scratch[0:D, s * GH * P:(s + 1) * GH * P] for s in range(2)]
        rT = [scratch[:, (2 + s) * GH * P:(3 + s) * GH * P] for s in range(2)]
        X = [work, cur]
        Y = [cur, work]
        A = [work[0:RP, i * RW:(i + 1) * RW] for i in range(3)]
        B = [cur[0:RP, i * RW:(i + 1) * RW] for i in range(3)]
        U = [t[0:RP, 0:RW // 2].bitcast(u16) for t in (logit, ga, gb, rowf)]
        hi_one_hot = [t[:, 0:2 * CH * HI].rearrange("p (h k n) -> p h k n", h=2, k=CH) for t in Y]
        lo_weighted = [t[:, 2400:2400 + 2 * SE].rearrange("p (h k n) -> p h k n", h=2, k=CH) for t in Y]
        lo_one_hot = [t[:, 4480:4480 + SE].bitcast(bf16).rearrange("p (h n k) -> p h n k", h=2, k=CH) for t in Y]

        edges_padded, constants_ready, weights_loaded, x_loaded = sem("edges_padded"), sem("constants_ready"), sem("weights_loaded"), sem("x_loaded")
        rows_loaded, cols_loaded, noise_loaded = sem("rows_loaded"), sem("cols_loaded"), sem("noise_loaded")
        u16_ready, u16_stored = sem("u16_ready"), sem("u16_stored")
        rows_split, chunks_transposed, transposes_kept = sem("rows_split"), sem("chunks_transposed"), sem("transposes_kept")
        dve_step, dve_to_act, act_to_dve = sem("dve_step"), sem("dve_to_act"), sem("act_to_dve")
        residual_ready, residual_stored = sem("residual_ready"), sem("residual_stored")
        group_staged, x_piece_ready = sem("group_staged"), sem("x_piece_ready")
        group_transposed, hT_ready, hidden_multiplied, rT_ready, scores_ready, scores_kept = (sem(n) for n in ("group_transposed", "hT_ready", "hidden_multiplied", "rT_ready", "scores_ready", "scores_kept"))
        parts_ready, mask_ready = sem("parts_ready"), sem("mask_ready")
        lo_loaded = [sem("lo_loaded_r"), sem("lo_loaded_c")]
        one_hot_ready = [sem("one_hot_ready_r"), sem("one_hot_ready_c")]
        gathered = [sem("gathered_r"), sem("gathered_c")]
        selected = [sem("selected_r"), sem("selected_c")]
        hi_one_hot_ready = sem("hi_one_hot_ready")
        lo_one_hot_ready, sums_added, row_sums_ready = sem("lo_one_hot_ready"), sem("sums_added"), sem("row_sums_ready")
        y_ready, y_stored = sem("y_ready"), sem("y_stored")
        weighted_by_act, weighted_by_dve = sem("weighted_by_act"), sem("weighted_by_dve")
        dist_ready, logits_ready, sigmoid_ready, gather_index_ready, fetched_kept = (sem(n) for n in ("dist_ready", "logits_ready", "sigmoid_ready", "gather_index_ready", "fetched_kept"))
        a_fetched = [sem("a_fetched0"), sem("a_fetched1")]
        a_ready, a_stored = sem("a_ready"), sem("a_stored")
        span_ready, widest_ready, local_ready, bases_stored, bases_loaded, b_ready, b_stored = (sem(n) for n in ("span_ready", "widest_ready", "local_ready", "bases_stored", "bases_loaded", "b_ready", "b_stored"))
        near_rows_loaded, near_cols_loaded, near_b_loaded, msg_cols_loaded, y_window_loaded = ([sem(f"{n}{h}") for h in range(2)] for n in ("near_rows_loaded", "near_cols_loaded", "near_b_loaded", "msg_cols_loaded", "y_window_loaded"))
        far_cols_loaded = [sem(f"far_cols_loaded{v}") for v in range(FAR // 2)]
        far_b_loaded = [sem(f"far_b_loaded{u}") for u in range(FAR)]
        window_one_hot_ready, y_spread, y_kept = sem("window_one_hot_ready"), sem("y_spread"), sem("y_kept")
        tables_cleared = [sem("tables_cleared0"), sem("tables_cleared1")]
        msg_rows_loaded = [sem("msg_rows_loaded0"), sem("msg_rows_loaded1")]
        count_step, scatter_index_ready, merge_ready, merged, message_ready = (sem(n) for n in ("count_step", "scatter_index_ready", "merge_ready", "merged", "message_ready"))
        y_fetched = [sem("y_fetched0"), sem("y_fetched1")]
        table_added = [sem(f"table_added{k}") for k in range(CH)]
        table_loaded = [sem(f"table_loaded{k}") for k in range(4)]
        residual_loaded, finish_step = sem("residual_loaded"), sem("finish_step")
        table_summed, output_piece_ready, output_stored = sem("table_summed"), sem("output_piece_ready"), sem("output_stored")

        def slot(u):
            return u % GP % 2

        def lag(u):
            return 1 if u % GP == 0 else 2

        def wait(eng, semaphore, value):
            if not isinstance(value, int) or value > 0:
                eng.wait_ge(semaphore, value)

        def steps(eng, first, end, body):
            body(first)
            with eng.Fori(first + 1, end - 1) as i:
                body(i)
            body(end - 1)

        far_bc = (row_bc[:, :, :], lo_bc[:, :, :], ones_lo[:, :, :].bitcast(u16))

        def rows_dma(eng, dram, tile, width, total, semaphore):
            full = total // width
            cut = full // 16 * 16
            for a, b in ((0, cut), (cut, full)):
                eng.dma_start(tile[a:b, 0:width], dram[a * width:b * width].rearrange("(p f) -> p f", f=width)).then_inc(semaphore, 16)
            rest = total - full * width
            eng.dma_start(tile[full:full + 1, 0:rest], dram[full * width:total].rearrange("(p f) -> p f", p=1)).then_inc(semaphore, 16)

        xv = x.rearrange("n d -> (n d)")
        block = ctx.enter_context(nc.Block())

        @block.sync
        def _(sp):
            sp.wait_ge(edges_padded, 1)
            rows_dma(sp, src, A[0].bitcast(i32), RW, E, rows_loaded)
            sp.wait_ge(edges_padded, 2)
            rows_dma(sp, dst, A[1].bitcast(i32), RW, E, cols_loaded)
            sp.wait_ge(edges_padded, 3)
            rows_dma(sp, noise.rearrange("e o -> (e o)"), A[2], RW, E, noise_loaded)
            for L, (nbW, nbb, selfW, selfb, attW, attbias) in enumerate(params):
                sp.dma_start(W[L][:, 0:D], nbW).then_inc(weights_loaded, 16)
                sp.dma_start(W[L][:, D:2 * D], selfW).then_inc(weights_loaded, 16)
                sp.dma_start(bias[L][0:D, :], nbb.rearrange("(d o) -> d o", o=1)).then_inc(weights_loaded, 16)
                sp.dma_start(bias[L][D:P, :], selfb.rearrange("(d o) -> d o", o=1)).then_inc(weights_loaded, 16)
                sp.wait_ge(edges_padded, 4)
                sp.dma_start(att[L][0:D, 0:1], attW[0:D, :]).then_inc(weights_loaded, 16)
                sp.dma_start(att[L][D:P, 1:2], attW[D:2 * D, :]).then_inc(weights_loaded, 16)
                sp.dma_start(attb[L][:, :], attbias.rearrange("(a o) -> a o", o=1).to_broadcast([P, 1])).then_inc(weights_loaded, 16)
            for n, (d, u) in enumerate(((row_d, U[0]), (rlo_d, U[1]), (crel_d, U[3]), (clo_d, U[2]))):
                sp.wait_ge(u16_ready, n + 1)
                sp.dma_start(d.rearrange("(p f) -> p f", p=RP), u).then_inc(u16_stored, 16)
            sp.wait_ge(span_ready, 1)
            sp.dma_start(base_d.rearrange("(p j) -> p j", p=RP), span[0:RP, 2, :].bitcast(i32)).then_inc(bases_stored, 16)
            sp.wait_ge(bases_stored, 16)
            sp.dma_start(bases[:, :], base_d.rearrange("(o n) -> o n", o=1)).then_inc(bases_loaded, 16)
            sp.wait_ge(rows_split, 4)
            rows_dma(sp, xv, cur, HI * D, N * D, x_loaded)

            def clear(L, k, part):
                t = tab_d[L][k].rearrange("(p r) d -> p (r d)", p=P)
                sp.dma_start(t[:, bass.ds(part * ZW, ZW)], zero[:, :]).then_inc(tables_cleared[L], 16)
            sp.wait_ge(constants_ready, 9)
            for k in range(CH):
                for part in range(8):
                    clear(0, k, part)
            sp.wait_ge(residual_ready, 1)
            sp.dma_start(acc_d, cur[:, :]).then_inc(residual_stored, 16)
            sp.wait_ge(u16_stored, 64)
            sp.wait_ge(bases_loaded, 16)
            sp.wait_ge(local_ready, 1)
            is_local = sp.value_load(local[0:1, 0:1], min_val=0, max_val=1)

            def window(t):
                return sp.value_load(bases[0:1, bass.ds(t, 1)], min_val=0, max_val=NP - P)

            def spread(d, t):
                return d[bass.ds(t * SE, SE)].rearrange("(o f) -> o f", o=1).to_broadcast([P, SE])

            for L in range(2):
                base = L * NS
                sp.wait_ge(b_ready, L + 1)
                sp.dma_start(b_d[L].rearrange("(p f) o -> p (f o)", p=P), b_out[:, :, :].rearrange("p f o -> p (f o)")).then_inc(b_stored, 16)
                sp.wait_ge(b_stored, 16 * (L + 1))
                sp.wait_ge(a_ready, L + 1)
                sp.dma_start(a_d[L][0:NP, :].rearrange("(p f) o -> p (f o)", p=P), a_out[:, :]).then_inc(a_stored, 16)
                sp.dma_start(a_d[L][NP:NP + 1, :], zero[0:1, 0:1]).then_inc(a_stored, 16)

                def load_lo(i):
                    for t, d in enumerate((rlo_d, clo_d)):
                        wait(sp, one_hot_ready[t], base + i)
                        sp.dma_start(lo_bc[:, t, :], d[bass.ds(i * SE, SE)].rearrange("(o f) -> o f", o=1).to_broadcast([P, SE])).then_inc(lo_loaded[t], 16)

                def load_cols_local(i):
                    later = not isinstance(i, int) or i > NA // FAR
                    for v, pair in enumerate(far_bc):
                        t = i * FAR + 2 * v
                        if later:
                            sp.wait_ge(one_hot_ready[1], base + t - FAR + 2)
                        sp.dma_start(pair.rearrange("p h e -> p (h e)"),
                                     crel_d[bass.ds(t * SE, 2 * SE)].rearrange("(o f) -> o f", o=1).to_broadcast([P, 2 * SE])).then_inc(far_cols_loaded[v], 16)
                        if later:
                            sp.wait_ge(gathered[1], base + t - FAR + 1)
                        sp.dma_start(b_window[:, 2 * v, 0:3], b_d[L][bass.ds(window(t), P), :]).then_inc(far_b_loaded[2 * v], 16)

                def load_lo_local(i):
                    for h in range(2):
                        t = i * 2 + h
                        wait(sp, one_hot_ready[0], L * NA + t - 1)
                        sp.dma_start(lo_bc[:, h, :], spread(rlo_d, t)).then_inc(near_rows_loaded[h], 16)
                        wait(sp, one_hot_ready[1], base + t - 1)
                        sp.dma_start(row_bc[:, h, :], spread(crel_d, t)).then_inc(near_cols_loaded[h], 16)
                        wait(sp, gathered[1], base + t - 1)
                        sp.dma_start(b_window[:, h, 0:3], b_d[L][bass.ds(window(t), P), :]).then_inc(near_b_loaded[h], 16)
                with sp.If(is_local):
                    steps(sp, 0, NA // 2, load_lo_local)
                    sp.wait_ge(one_hot_ready[0], NA * (L + 1))
                    sp.wait_ge(one_hot_ready[1], base + NA)
                    sp.wait_ge(gathered[1], base + NA)
                    sp.wait_ge(gathered[0], NA * (L + 1))
                    steps(sp, NA // FAR, NS // FAR, load_cols_local)
                with sp.Else():
                    steps(sp, 0, NS, load_lo)

                def store_y():
                    for p_ in range(YP):
                        a, b = p_ * YW, (p_ + 1) * YW
                        sp.wait_ge(y_ready, L * YP + p_ + 1)
                        sp.dma_start(y_d[L].rearrange("(p f) d -> p (f d)", p=P)[:, a:b], Y[L][:, a:b]).then_inc(y_stored, 16)
                    sp.wait_ge(y_stored, 16 * YP * (L + 1))

                def load_row(i):
                    for h in range(2):
                        wait(sp, merge_ready, base + i * 2 + h - 1)
                        sp.dma_start(row_bc[:, h, :], row_d[bass.ds((i * 2 + h) * SE, SE)].rearrange("(o f) -> o f", o=1).to_broadcast([P, SE])).then_inc(msg_rows_loaded[h], 16)

                def load_row_local(i):
                    for h in range(2):
                        t = i * 2 + h
                        wait(sp, merge_ready, base + t - 1)
                        sp.dma_start(row_bc[:, h, :], spread(row_d, t)).then_inc(msg_rows_loaded[h], 16)
                        wait(sp, window_one_hot_ready, base + t - 1)
                        sp.dma_start(lo_bc[:, h, :], spread(crel_d, t)).then_inc(msg_cols_loaded[h], 16)
                        if isinstance(i, int) and i == 0 and h == 0:
                            store_y()
                        wait(sp, y_spread, base + t - 1)
                        sp.dma_start(y_window[:, h, :], y_d[L][bass.ds(window(t), P), :]).then_inc(y_window_loaded[h], 16)
                with sp.If(is_local):
                    sp.wait_ge(one_hot_ready[1], base + NS)
                    if L == 0:
                        load_row_local(0)
                        for k in range(CH):
                            with sp.Fori(1 + 8 * k, 9 + 8 * k) as i:
                                load_row_local(i)
                                clear(1, k, i - (1 + 8 * k))
                        with sp.Fori(1 + 8 * CH, NS // 2) as i:
                            load_row_local(i)
                    else:
                        steps(sp, 0, NS // 2, load_row_local)
                with sp.Else():
                    store_y()
                    if L == 0:
                        for k in range(CH):
                            for part in range(8):
                                clear(1, k, part)
                    steps(sp, 0, NS // 2, load_row)
                for k in range(CH):
                    sp.wait_ge(table_added[k], 16 * NS * (L + 1))
                sp.wait_ge(y_stored, 16 * YP * (L + 1))

                def load_piece(i):
                    for k in range(CH):
                        wait(sp, table_summed, (L * PIECES + i) * CH + k - 3)
                        t = tab_d[L][k][0:NP, :].rearrange("(p f) d -> p (f d)", p=P)
                        sp.dma_start(work[:, (k % 4) * PW:(k % 4 + 1) * PW], t[:, bass.ds(i * PW, PW)]).then_inc(table_loaded[k % 4], 16)
                    if L == 1:
                        wait(sp, output_piece_ready, i)
                        sp.dma_start(work[:, 5 * PW:6 * PW], acc_d[:, bass.ds(i * PW, PW)]).then_inc(residual_loaded, 16)
                steps(sp, 0, PIECES, load_piece)

        @block.gpsimd
        def _(pool):
            pool.iota(iota[:, :], [[1, HI]], base=0, channel_multiplier=0, allow_small_or_imprecise_dtypes=True).then_inc(constants_ready, 1)
            pool.iota(pid[:, :], [[0, 1]], base=0, channel_multiplier=1, allow_small_or_imprecise_dtypes=True).then_inc(constants_ready, 1)
            pool.iota(npid[:, :], [[0, 1]], base=0, channel_multiplier=-1, allow_small_or_imprecise_dtypes=True).then_inc(constants_ready, 1)
            pool.iota(trash[:, :], [[0, 1]], base=NP, channel_multiplier=1, allow_small_or_imprecise_dtypes=True).then_inc(constants_ready, 1)
            pool.memset(ident[:, :], 0.0).then_inc(constants_ready, 1)
            pool.memset(earlier[:, :], 1.0).then_inc(constants_ready, 1)
            pool.memset(zero[:, :], 0.0).then_inc(constants_ready, 1)
            pool.memset(eps[:, 0:1], EPS_LN).then_inc(constants_ready, 1)
            pool.memset(eps[:, 1:2], EPS_DEG).then_inc(constants_ready, 1)
            pool.wait_ge(constants_ready, 9)
            pool.affine_select(out=ident[:, :], in_=ident[:, :], compare_op=ALU.not_equal, fill=1.0, base=0,
                               pattern=[[-1, P]], channel_multiplier=1).then_inc(constants_ready, 1)
            pool.affine_select(out=earlier[:, :], in_=earlier[:, :], compare_op=ALU.is_gt, fill=0.0, base=0,
                               pattern=[[-1, P]], channel_multiplier=1).then_inc(constants_ready, 1)
            pool.wait_ge(span_ready, 2)
            pool.partition_all_reduce(wide[:, 1:2], wide[:, 0:1], P, bass.bass_isa.ReduceOp.max).then_inc(widest_ready, 1)
            pool.wait_ge(local_ready, 1)
            is_local = pool.value_load(local[0:1, 0:1], min_val=0, max_val=1)
            for L in range(2):
                base = L * NS
                mine = L * NB
                pool.wait_ge(a_stored, 32 * (L + 1))

                def prepare(i, h):
                    pool.tensor_copy(aidx[:, h, :], rowf[:, bass.ds((i * 2 + h + NA) * CH, CH)]).then_inc(gather_index_ready, 1)

                def keep(i, h):
                    pool.wait_ge(a_fetched[h], (mine // 2 + i + 1) * 16 * CH)
                    pool.tensor_copy(ga[:, bass.ds((i * 2 + h + NA) * CH, CH)], arow[:, h, :]).then_inc(fetched_kept, 1)

                def fetch(i, last=False):
                    for h in range(2):
                        pool.wait_ge(gather_index_ready, mine + i * 2 + h + 1)
                        wait(pool, fetched_kept, mine + i * 2 + h - 1)
                        pool.nop(nofuse=True)
                        for k in range(CH):
                            pool.indirect_dma_start(
                                out=arow[:, h, k:k + 1], out_offset=None, in_=a_d[L],
                                in_offset=bass.IndirectOffsetOnAxis(ap=aidx[:, h, k:k + 1], axis=0)).then_inc(a_fetched[h], 16)
                        if h == 1 or not isinstance(i, int) or i > 0:
                            keep(i - 1 + h, 1 - h)
                        if not (last and h == 1):
                            prepare(i + h, 1 - h)
                with pool.If(is_local):
                    prepare(0, 0)
                    fetch(0)
                    with pool.Fori(1, NB // 2 - 1) as i:
                        fetch(i)
                    fetch(NB // 2 - 1, True)
                    keep(NB // 2 - 1, 1)
                with pool.Else():
                    pool.nop()
                pool.wait_ge(y_stored, 16 * YP * (L + 1))
                pool.wait_ge(tables_cleared[L], 16 * CH * 8)

                def add_messages(t, u):
                    pool.wait_ge(message_ready, base + t + 1)
                    for k in range(CH):
                        wait(pool, table_added[k], (base + t) * 16)
                        pool.nop(nofuse=True)
                        pool.indirect_dma_start(
                            out=tab_d[L][k], out_offset=bass.IndirectOffsetOnAxis(ap=ridx[:, u, k:k + 1], axis=0),
                            in_=msg[:, u, k, :], in_offset=None, compute_op=ALU.add).then_inc(table_added[k], 16)

                def body_local(i):
                    for u in range(4):
                        pool.wait_ge(scatter_index_ready, base + i * 4 + u + 1)
                        add_messages(i * 4 + u, u)

                def body(i):
                    for u in range(4):
                        h = u % 2
                        t = i * 4 + u
                        pool.wait_ge(scatter_index_ready, base + t + 1)
                        wait(pool, merged, base + t - 1)
                        pool.nop(nofuse=True)
                        for k in range(CH):
                            pool.indirect_dma_start(
                                out=y_edge[:, h, k, :], out_offset=None, in_=y_d[L],
                                in_offset=bass.IndirectOffsetOnAxis(ap=cidx[:, h, k:k + 1], axis=0)).then_inc(y_fetched[h], 16)
                        add_messages(t, u)
                with pool.If(is_local):
                    steps(pool, 0, NS // 4, body_local)
                with pool.Else():
                    steps(pool, 0, NS // 4, body)
            for k in range(CH):
                pool.wait_ge(table_added[k], 16 * NS * 2)

        @block.scalar
        def _(act):
            act.wait_ge(constants_ready, 9)
            act.wait_ge(dve_to_act, 1)
            act.activation(logit[:, :], ga[:, :], ACT.Ln).then_inc(act_to_dve, 1)
            act.activation(gb[:, :], ga[:, :], ACT.Ln, bias=1.0, scale=-1.0).then_inc(act_to_dve, 1)

            def deviations(p_):
                act.wait_ge(dve_to_act, 2 + p_)
                act.activation(st[:, 1, :], st[:, 0, :], ACT.Sqrt, bias=eps[:, 0:1], scale=1.0 / D).then_inc(act_to_dve, 1)
            deviations(0)
            act.wait_ge(weights_loaded, 16 * 14)
            act.wait_ge(constants_ready, 11)
            act.wait_ge(local_ready, 1)
            is_local = act.value_load(local[0:1, 0:1], min_val=0, max_val=1)
            for L in range(2):
                base = L * NS

                def stage(p_, u):
                    n = L * NG + p_ * GP + u
                    wait(act, group_transposed, n + 1 - lag(u))
                    act.activation(x_staged[:, slot(u), :], X[L][:, bass.ds((p_ * GP + u) * (GH * D), GH * D)], ACT.Copy).then_inc(group_staged, 1)

                def transposed(p_, u):
                    n = L * NG + p_ * GP + u
                    act.wait_ge(group_transposed, n + 1)
                    wait(act, hidden_multiplied, n + 1 - lag(u))
                    act.activation(hT[slot(u)], psG[0:D, slot(u), 0:GH * P], ACT.Copy).then_inc(hT_ready, 1)

                def hidden(p_, u):
                    n = L * NG + p_ * GP + u
                    act.wait_ge(hidden_multiplied, n + 1)
                    wait(act, scores_ready, n + 1 - lag(u))
                    act.activation(rT[slot(u)], psG[:, 2 + slot(u), 0:GH * P], ACT.Relu, bias=bias[L][:, 0:1]).then_inc(rT_ready, 1)

                def keep_ab(p_, u):
                    g = p_ * GP + u
                    act.wait_ge(scores_ready, L * NG + g + 1)
                    act.activation(ab[:, bass.ds(g * GH, GH), :].rearrange("p h t -> p (h t)"),
                                   psG[:, 4 + slot(u), 0:2 * GH], ACT.Copy).then_inc(scores_kept, 1)

                def node_piece(p_):
                    last = isinstance(p_, int) and p_ == PIECES - 1
                    for u in range(GP):
                        if not last and u == GP - 2:
                            if L == 0:
                                deviations(p_ + 1)
                            act.wait_ge(x_piece_ready, L * PIECES + p_ + 2)
                        if not (last and u >= GP - 2):
                            stage(p_, u + 2)
                        if not (last and u == GP - 1):
                            transposed(p_, u + 1)
                        hidden(p_, u)
                        if not isinstance(p_, int) or p_ * GP + u > 0:
                            keep_ab(p_, u - 1)
                act.wait_ge(x_piece_ready, L * PIECES + 1)
                stage(0, 0)
                stage(0, 1)
                transposed(0, 0)
                steps(act, 0, PIECES, node_piece)
                keep_ab(PIECES - 1, GP - 1)

                def col_one_hot(i):
                    for h in range(2):
                        t = i * 2 + h
                        act.wait_ge(near_cols_loaded[h], (L * NA // 2 + i + 1) * 16)
                        wait(act, one_hot_ready[1], base + t)
                        act.activation(dist, row_bc[:, h, :], ACT.Abs, bias=npid[:, 0:1]).then_inc(dist_ready, 1)
                        act.wait_ge(dist_ready, L * NA + t + 1)
                        wait(act, gathered[1], base + t - 1)
                        act.activation(window_one_hot[:, h, :], dist, ACT.Relu, bias=1.0, scale=-1.0).then_inc(one_hot_ready[1], 1)
                with act.If(is_local):
                    steps(act, 0, NA // 2, col_one_hot)
                with act.Else():
                    act.nop()

                def weigh(i):
                    for h in range(2):
                        t = i * 2 + h
                        act.wait_ge(lo_one_hot_ready, base + t + 1)
                        wait(act, sums_added, base + t - 1)
                        for k in range(CH - 1):
                            act.activation(lo_weighted[L][:, h, k, :], lo_one_hot[L][:, h, :, k], ACT.Copy,
                                           scale=ga[:, bass.ds(t * CH + k, 1)]).then_inc(weighted_by_act, 1)
                def load_windows(i):
                    for u in range(1, FAR, 2):
                        t = i * FAR + u
                        if not isinstance(i, int) or i > NA // FAR:
                            act.wait_ge(gathered[1], base + t - FAR + 1)
                        first = act.value_load(bases[0:1, bass.ds(t, 1)], min_val=0, max_val=NP - P)
                        act.dma_start(b_window[:, u, 0:3], b_d[L][bass.ds(first, P), :]).then_inc(far_b_loaded[u], 16)
                for part, (a, b) in enumerate(PARTS):
                    if part == 1:
                        with act.If(is_local):
                            act.wait_ge(gathered[1], base + NA)
                            steps(act, NA // FAR, NS // FAR, load_windows)
                        with act.Else():
                            act.nop()
                    act.wait_ge(logits_ready, len(PARTS) * L + part + 1)
                    act.activation(gb[:, a * CH:b * CH], ga[:, a * CH:b * CH], ACT.Sigmoid).then_inc(sigmoid_ready, 1)
                    act.wait_ge(mask_ready, len(PARTS) * L + part + 1)
                    steps(act, a // 2, b // 2, weigh)
                act.wait_ge(dve_to_act, 2 + PIECES + L)
                act.activation(dinv[:, :], abr[:, 0, :], ACT.Sqrt).then_inc(act_to_dve, 1)

                def messages(t, u):
                    act.wait_ge(merged, base + t + 1)
                    for k in range(CH):
                        wait(act, table_added[k], (base + t - 3) * 16)
                    act.activation(msg[:, u, :, :].rearrange("p k d -> p (k d)"), psG[:, u % 2, :], ACT.Copy).then_inc(message_ready, 1)

                def body(i):
                    for u in range(4):
                        messages(i * 4 + u, u)

                def body_local(i):
                    for u in range(4):
                        t, h = i * 4 + u, u % 2
                        act.wait_ge(y_spread, base + t + 1)
                        wait(act, merged, base + t - 1)
                        act.activation(y_edge[:, h, :, :].rearrange("p k d -> p (k d)"), psG[:, 2 + h, :], ACT.Copy).then_inc(y_kept, 1)
                        messages(t, u)
                with act.If(is_local):
                    steps(act, 0, NS // 4, body_local)
                with act.Else():
                    steps(act, 0, NS // 4, body)
            full = N // HI
            cut = full // 16 * 16
            flat = out.rearrange("n d -> (n d)")
            main = flat[0:full * HI * D].rearrange("(p f) -> p f", f=HI * D)

            def store_piece(i):
                act.wait_ge(output_piece_ready, i + 1)
                for a, b in ((0, cut), (cut, full)):
                    act.dma_start(main[a:b, bass.ds(i * PW, PW)], cur[a:b, bass.ds(i * PW, PW)]).then_inc(output_stored, 16)
            steps(act, 0, PIECES, store_piece)
            tail = (N - full * HI) * D
            act.dma_start(flat[full * HI * D:N * D].rearrange("(p f) -> p f", p=1), cur[full:full + 1, 0:tail]).then_inc(output_stored, 16)
            act.wait_ge(output_stored, 16 * (2 * PIECES + 1))

        @block.vector
        def _(dve):
            chained = [0]

            def link(ins):
                chained[0] += 1
                ins.then_inc(dve_step, 1)
                dve.wait_ge(dve_step, chained[0])

            dve.memset(A[0].bitcast(i32), PAD_ROW).then_inc(edges_padded, 1)
            dve.memset(A[1].bitcast(i32), N - 1).then_inc(edges_padded, 1)
            dve.memset(A[2], 0.5).then_inc(edges_padded, 1)
            dve.memset(att[0][:, :], 0.0)
            dve.memset(att[1][:, :], 0.0).then_inc(edges_padded, 1)

            def split(a, q, r):
                link(dve.tensor_scalar(q.bitcast(i32), a, 1.0 / HI, None, ALU.mult))
                link(dve.tensor_copy(q, q.bitcast(i32)))
                link(dve.scalar_tensor_tensor(r, q, -float(HI), a, ALU.mult, ALU.add))
                link(dve.scalar_tensor_tensor(q, r, 0.0, q, ALU.is_lt, ALU.subtract))
                link(dve.scalar_tensor_tensor(q, r, float(HI), q, ALU.is_ge, ALU.subtract))
                link(dve.scalar_tensor_tensor(a, q, -float(HI), a, ALU.mult, ALU.add))

            dve.wait_ge(rows_loaded, 48)
            link(dve.tensor_copy(A[0], A[0].bitcast(i32)))
            dve.tensor_copy(U[0], A[0]).then_inc(u16_ready, 1)
            split(A[0], B[0], B[2])
            dve.tensor_copy(U[1], B[0]).then_inc(u16_ready, 1)
            dve.wait_ge(cols_loaded, 48)
            link(dve.tensor_copy(A[1], A[1].bitcast(i32)))
            cols = A[1].rearrange("p (j e) -> p j e", j=RJ)
            link(dve.memset(wide[:, :], 0.0))
            link(dve.tensor_reduce(span[0:RP, 0, :], cols, AX.X, ALU.min))
            link(dve.tensor_scalar(span[0:RP, 0, :], span[0:RP, 0, :], float(NP - P), None, ALU.min))
            link(dve.tensor_reduce(span[0:RP, 1, :], cols, AX.X, ALU.max))
            link(dve.tensor_tensor(span[0:RP, 1, :], span[0:RP, 1, :], span[0:RP, 0, :], ALU.subtract))
            dve.tensor_copy(span[0:RP, 2, :].bitcast(i32), span[0:RP, 0, :]).then_inc(span_ready, 1)
            dve.tensor_reduce(wide[0:RP, 0:1], span[0:RP, 1, :], AX.X, ALU.max).then_inc(span_ready, 1)
            dve.tensor_tensor(U[3].rearrange("p (j e) -> p j e", j=RJ), cols, span[0:RP, 0, :].unsqueeze(2).to_broadcast([RP, RJ, SE]), ALU.subtract).then_inc(u16_ready, 1)
            dve.wait_ge(u16_ready, 3)
            split(A[1], B[1], B[2])
            dve.tensor_copy(U[2], B[1]).then_inc(u16_ready, 1)
            dve.wait_ge(noise_loaded, 48)
            dve.tensor_copy(B[2][:, 0:1], B[2][:, 0:1]).then_inc(rows_split, 1)
            dest = [lof, hif, rowf, chif, gb]
            n = 0
            for a, d in enumerate(dest):
                dv = d[:, :].rearrange("q (p j k) -> q j k p", j=RJ, k=CH)
                for j in range(RJ):
                    for kk in range(2):
                        dve.wait_ge(chunks_transposed, n + 1)
                        if a == 2 and j == 0 and kk == 0:
                            dve.wait_ge(u16_stored, 64)
                        dve.tensor_copy(dv[:, j, 4 * kk:4 * kk + 4, :],
                                        psG[:, n % 6, 0:4 * RP].rearrange("q (k p) -> q k p", k=4)).then_inc(transposes_kept, 1)
                        n += 1
            dve.wait_ge(transposes_kept, n)
            link(dve.scalar_tensor_tensor(coli[:, :], rowf[:, :], float(HI), chif[:, :], ALU.mult, ALU.add))
            link(dve.scalar_tensor_tensor(rowf[:, :], lof[:, :], float(HI), hif[:, :], ALU.mult, ALU.add))
            dve.tensor_scalar(ga[:, :], gb[:, :], EPS_NOISE, 1.0 - EPS_NOISE, ALU.max, ALU.min).then_inc(dve_to_act, 1)
            dve.wait_ge(act_to_dve, 2)
            link(dve.tensor_tensor(logit[:, :], logit[:, :], gb[:, :], ALU.subtract))
            dve.wait_ge(widest_ready, 1)
            dve.tensor_scalar(local[:, :], wide[:, 1:2], float(P - 1), None, ALU.is_le).then_inc(local_ready, 1)
            dve.wait_ge(local_ready, 1)
            is_local = dve.value_load(local[0:1, 0:1], min_val=0, max_val=1)
            link(dve.memset(cur[96:P, :], 0.0))
            dve.sem_inc(rows_split, 3)
            dve.wait_ge(x_loaded, 48)
            dve.wait_ge(constants_ready, 11)
            dve.tensor_copy(iota8[:, :, :], iota[:, 0:P].unsqueeze(2).to_broadcast([P, P, CH]))
            for p_ in range(PIECES):
                def piece(t):
                    return t[:, p_ * PW:(p_ + 1) * PW].rearrange("p (h d) -> p h d", d=D)
                sq = merge[:, :, :, :].rearrange("p a k n -> p (a k n)")[:, 0:PW].rearrange("p (h d) -> p h d", d=D)
                s0, s1 = st[:, 0, :], st[:, 1, :]
                link(dve.tensor_reduce(s0, piece(cur), AX.X, ALU.add))
                link(dve.tensor_scalar(s1, s0, 1.0 / D, None, ALU.mult))
                link(dve.tensor_tensor(piece(work), piece(cur), s1.unsqueeze(2).to_broadcast([P, PH, D]), ALU.subtract))
                link(dve.tensor_tensor(sq, piece(work), piece(work), ALU.mult))
                dve.tensor_reduce(s0, sq, AX.X, ALU.add).then_inc(dve_to_act, 1)
                dve.wait_ge(act_to_dve, 3 + p_)
                link(dve.reciprocal(s0, s1))
                link(dve.tensor_tensor(piece(work), piece(work), s0.unsqueeze(2).to_broadcast([P, PH, D]), ALU.mult))
                dve.tensor_scalar(piece(work), piece(work), 0.0, None, ALU.max).then_inc(x_piece_ready, 1)
                dve.wait_ge(x_piece_ready, p_ + 1)
                link(dve.tensor_tensor(piece(cur), piece(cur), piece(work), ALU.add))
            dve.sem_inc(residual_ready, 1)

            for L in range(2):
                base = L * NS

                dve.wait_ge(scores_kept, NG * (L + 1))
                abv = ab[:, :, :].rearrange("p h t -> p t h")
                link(dve.tensor_copy(ab_parts[:, 0, :, :], abv))
                link(dve.tensor_tensor(abr[:, :, :], abv, ab_parts[:, 0, :, :], ALU.subtract))
                link(dve.tensor_copy(ab_parts[:, 1, :, :], abr[:, :, :]))
                link(dve.tensor_tensor(abr[:, :, :], abr[:, :, :], ab_parts[:, 1, :, :], ALU.subtract))
                dve.tensor_copy(ab_parts[:, 2, :, :], abr[:, :, :]).then_inc(parts_ready, 1)
                dve.wait_ge(parts_ready, L + 1)
                dve.tensor_copy(a_out[:, :], ab[:, :, 0]).then_inc(a_ready, 1)
                dve.tensor_copy(b_out[:, :, :], ab_parts[:, :, 1, :].rearrange("p m h -> p h m")).then_inc(b_ready, 1)

                def one_hot(t, i):
                    dve.wait_ge(lo_loaded[t], (base + i + 1) * 16)
                    wait(dve, gathered[t], base + i)
                    dve.tensor_scalar(ones_lo[:, t, :], lo_bc[:, t, :], pid[:, 0:1], None, ALU.is_equal).then_inc(one_hot_ready[t], 1)

                def select(t, i):
                    dve.wait_ge(gathered[t], base + i + 1)
                    wait(dve, selected[t], base + i)
                    for k in range(CH):
                        c = i * CH + k
                        ins = dve.scalar_tensor_tensor(
                            junk[t][:, k, :], iota[:, :], (hif, chif)[t][:, bass.ds(c, 1)],
                            psG[:, 3 * t + k // 3, (k % 3) * HI:(k % 3 + 1) * HI], ALU.is_equal, ALU.mult,
                            accum_out=(ga, gb)[t][:, bass.ds(c, 1)])
                    ins.then_inc(selected[t], 1)

                def gather(i, last=False):
                    one_hot(1, i)
                    select(0, i)
                    if not last:
                        one_hot(0, i + 1)
                    select(1, i)

                def row_one_hot(i, h):
                    dve.wait_ge(near_rows_loaded[h], (L * NA // 2 + i + 1) * 16)
                    wait(dve, gathered[0], L * NA + i * 2 + h - 1)
                    dve.tensor_scalar(ones_lo[:, h, :], lo_bc[:, h, :], pid[:, 0:1], None, ALU.is_equal).then_inc(one_hot_ready[0], 1)

                def gather_local(i, last=False):
                    for h in range(2):
                        t = i * 2 + h
                        if not (last and h == 1):
                            row_one_hot(i + h, 1 - h)
                        dve.wait_ge(gathered[0], L * NA + t + 1)
                        wait(dve, selected[0], L * NA + t)
                        for k in range(CH):
                            c = t * CH + k
                            ins = dve.scalar_tensor_tensor(
                                junk[0][:, k, :], iota[:, :], hif[:, bass.ds(c, 1)],
                                psG[:, 3 * h + k // 3, (k % 3) * HI:(k % 3 + 1) * HI], ALU.is_equal, ALU.mult,
                                accum_out=ga[:, bass.ds(c, 1)])
                        ins.then_inc(selected[0], 1)
                        col_values(t, psR[:, 0, 0:3 * CH])

                def col_values(t, parts):
                    dve.wait_ge(gathered[1], base + t + 1)
                    dve.tensor_reduce(gb[:, bass.ds(t * CH, CH)], parts.rearrange("p (k m) -> p k m", m=3), AX.X, ALU.add).then_inc(selected[1], 1)

                def gather_cols(i, last=False):
                    for u in range(FAR):
                        if not (last and u == FAR - 1):
                            far_one_hot(i + (u + 1) // FAR, (u + 1) % FAR)
                        col_values(i * FAR + u, psG[:, u % 2, 0:3 * CH])

                def far_one_hot(i, u):
                    dve.wait_ge(far_cols_loaded[u // 2], (i - NA // FAR + L * NB // FAR + 1) * 16)
                    wait(dve, gathered[1], base + i * FAR + u - 1)
                    dve.tensor_scalar(window_one_hot[:, u % 2, :], far_bc[u // 2][:, u % 2, :], pid[:, 0:1], None, ALU.is_equal).then_inc(one_hot_ready[1], 1)
                with dve.If(is_local):
                    row_one_hot(0, 0)
                    gather_local(0)
                    with dve.Fori(1, NA // 2 - 1) as i:
                        gather_local(i)
                    gather_local(NA // 2 - 1, True)
                    dve.wait_ge(selected[0], NA * (L + 1))
                    dve.wait_ge(selected[1], base + NA)
                with dve.Else():
                    one_hot(0, 0)
                    with dve.Fori(0, NS - 1) as i:
                        gather(i)
                    gather(NS - 1, True)
                    dve.wait_ge(selected[0], base + NS)
                    dve.wait_ge(selected[1], base + NS)

                def mask(part, a, b):
                    va, vb, vl = (t[:, a * CH:b * CH] for t in (ga, gb, logit))
                    link(dve.scalar_tensor_tensor(va, va, attb[L][:, 0:1], vb, ALU.add, ALU.add))
                    dve.tensor_tensor(va, va, vl, ALU.add).then_inc(logits_ready, 1)
                    dve.wait_ge(sigmoid_ready, len(PARTS) * L + part + 1)
                    link(dve.tensor_scalar(va, vb, ZETA - GAMMA, GAMMA, ALU.mult, ALU.add))
                    dve.tensor_scalar(va, va, 0.0, 1.0, ALU.max, ALU.min).then_inc(mask_ready, 1)
                    dve.wait_ge(mask_ready, len(PARTS) * L + part + 1)

                def scatter(i):
                    for h in range(2):
                        t = i * 2 + h
                        wait(dve, sums_added, base + t - 1)
                        dve.tensor_tensor(lo_one_hot[L][:, h, :, :], iota8[:, :, :],
                                          lof[:, bass.ds(t * CH, CH)].unsqueeze(1).to_broadcast([P, P, CH]), ALU.is_equal).then_inc(lo_one_hot_ready, 1)
                        dve.tensor_tensor(hi_one_hot[L][:, h, :, :], iota[:, :].unsqueeze(1).to_broadcast([P, CH, HI]),
                                          hif[:, bass.ds(t * CH, CH)].unsqueeze(2).to_broadcast([P, CH, HI]), ALU.is_equal).then_inc(hi_one_hot_ready, 1)
                        dve.wait_ge(lo_one_hot_ready, base + t + 1)
                        dve.tensor_scalar(lo_weighted[L][:, h, CH - 1, :], lo_one_hot[L][:, h, :, CH - 1], ga[:, bass.ds(t * CH + CH - 1, 1)],
                                          None, ALU.mult).then_inc(weighted_by_dve, 1)
                if L == 0:
                    dve.wait_ge(residual_stored, 16)
                mask(0, *PARTS[0])
                steps(dve, 0, NA // 2, scatter)
                with dve.If(is_local):
                    far_one_hot(NA // FAR, 0)
                    gather_cols(NA // FAR)
                    with dve.Fori(NA // FAR + 1, NS // FAR - 1) as i:
                        gather_cols(i)
                    gather_cols(NS // FAR - 1, True)
                    dve.wait_ge(selected[1], base + NS)
                with dve.Else():
                    dve.nop()
                for part in (1, 2):
                    a, b = PARTS[part]
                    with dve.If(is_local):
                        dve.wait_ge(fetched_kept, NB * L + b - NA)
                    with dve.Else():
                        dve.nop()
                    mask(part, a, b)
                    steps(dve, a // 2, b // 2, scatter)
                dve.wait_ge(row_sums_ready, L + 1)
                dve.tensor_scalar(abr[:, 0, :], psR[:, 1, 0:HI], EPS_DEG, None, ALU.add).then_inc(dve_to_act, 1)
                dve.wait_ge(act_to_dve, 3 + PIECES + L)
                link(dve.reciprocal(abr[:, 1, :], dinv[:, :]))
                link(dve.tensor_scalar(dinv[:, :], abr[:, 1, :], 0.0, 10.0, ALU.max, ALU.min))
                for p_ in range(YP):
                    def part(t):
                        return t[:, p_ * YW:(p_ + 1) * YW].rearrange("p (h d) -> p h d", d=D)
                    w = HI // YP
                    dve.tensor_tensor(part(Y[L]), part(X[L]), dinv[:, p_ * w:(p_ + 1) * w].unsqueeze(2).to_broadcast([P, w, D]),
                                      ALU.mult).then_inc(y_ready, 1)

                def body(i, by_window):
                    for u in range(4):
                        t, h = i * 4 + u, u % 2
                        c = t * CH
                        wait(dve, scatter_index_ready, base + t)
                        dve.wait_ge(msg_rows_loaded[h], (base // 2 + i * 2 + u // 2 + 1) * 16)
                        for k in range(CH):
                            dve.scalar_tensor_tensor(same[:, k, :], row_bc[:, h, k * P:(k + 1) * P], rowf[:, bass.ds(c + k, 1)],
                                                     earlier[:, :], ALU.is_equal, ALU.mult, accum_out=cnt[:, k:k + 1])
                        for k in range(CH):
                            wait(dve, table_added[k], (base + t - 3) * 16)
                        wait(dve, merged, base + t - 1)
                        dve.tensor_copy(cidx[:, h, :], coli[:, bass.ds(c, CH)])
                        dve.tensor_scalar(dtmp[:, :], rowf[:, bass.ds(c, CH)], -1.0, trash[:, 0:1], ALU.mult, ALU.add).then_inc(count_step, 1)
                        dve.wait_ge(count_step, (base + t) * 2 + 1)
                        dve.scalar_tensor_tensor(dtmp[:, :], cnt[:, :], 1.0, dtmp[:, :], ALU.min, ALU.mult).then_inc(count_step, 1)
                        dve.wait_ge(count_step, (base + t) * 2 + 2)
                        dve.tensor_tensor(ridx[:, u, :], dtmp[:, :], rowf[:, bass.ds(c, CH)], ALU.add).then_inc(scatter_index_ready, 1)
                        if by_window:
                            dve.wait_ge(msg_cols_loaded[h], (base // 2 + i * 2 + u // 2 + 1) * 16)
                            wait(dve, y_spread, base + t - 1)
                            dve.tensor_scalar(window_one_hot_f32[:, h, :], lo_bc[:, h, :], pid[:, 0:1], None, ALU.is_equal).then_inc(window_one_hot_ready, 1)
                        wait(dve, merged, base + t - 1)
                        for k in range(CH):
                            ins = dve.tensor_scalar(merge[:, h, k, :], row_bc[:, h, k * P:(k + 1) * P], rowf[:, bass.ds(c + k, 1)],
                                                    ga[:, bass.ds(c + k, 1)], ALU.is_equal, ALU.mult)
                        ins.then_inc(merge_ready, 1)
                with dve.If(is_local):
                    steps(dve, 0, NS // 4, lambda i: body(i, True))
                with dve.Else():
                    steps(dve, 0, NS // 4, lambda i: body(i, False))

                def combine(i):
                    S = work[:, 4 * PW:5 * PW]
                    C = cur[:, bass.ds(i * PW, PW)]
                    dv = dinv[:, bass.ds(i * PH, PH)].unsqueeze(2).to_broadcast([P, PH, D])

                    def by_node(t):
                        return t.rearrange("p (h d) -> p h d", d=D)
                    for k in range(CH):
                        n = (L * PIECES + i) * CH + k
                        dve.wait_ge(table_loaded[k % 4], 16 * ((L * PIECES + i) * 2 + k // 4 + 1))
                        T = work[:, (k % 4) * PW:(k % 4 + 1) * PW]
                        if k == 0:
                            if L == 0:
                                dve.wait_ge(x_piece_ready, PIECES + i)
                            dve.tensor_copy(S, T).then_inc(table_summed, 1)
                        else:
                            dve.tensor_tensor(S, S, T, ALU.add).then_inc(table_summed, 1)
                        dve.wait_ge(table_summed, n + 1)
                    if L == 0:
                        dve.tensor_tensor(by_node(C), by_node(S), dv, ALU.mult).then_inc(x_piece_ready, 1)
                    else:
                        dve.tensor_tensor(by_node(S), by_node(S), dv, ALU.mult).then_inc(finish_step, 1)
                        dve.wait_ge(residual_loaded, 16 * (i + 1))
                        dve.wait_ge(finish_step, i * 2 + 1)
                        dve.tensor_tensor(S, S, C, ALU.add).then_inc(finish_step, 1)
                        dve.wait_ge(finish_step, i * 2 + 2)
                        dve.tensor_tensor(C, S, work[:, 5 * PW:6 * PW], ALU.add).then_inc(output_piece_ready, 1)
                        dve.wait_ge(output_piece_ready, i + 1)
                steps(dve, 0, PIECES, combine)

        @block.tensor
        def _(pe):
            pe.wait_ge(constants_ready, 11)
            n = 0
            pe.wait_ge(rows_split, 1)
            for a in (B[0], A[0], B[1], A[1], A[2]):
                for j in range(RJ):
                    for kk in range(2):
                        if n >= 6:
                            pe.wait_ge(transposes_kept, n - 5)
                        for k in range(4):
                            f = (j * CH + kk * 4 + k) * P
                            ins = pe.transpose(psG[:, n % 6, k * RP:(k + 1) * RP], a[:, f:f + P], ident[0:RP, 0:RP])
                        ins.then_inc(chunks_transposed, 1)
                        n += 1
            pe.wait_ge(weights_loaded, 16 * 14)
            pe.wait_ge(local_ready, 1)
            is_local = pe.value_load(local[0:1, 0:1], min_val=0, max_val=1)
            for L in range(2):
                base = L * NS

                def transposes(p_, u):
                    n = L * NG + p_ * GP + u
                    wait(pe, hT_ready, n + 1 - lag(u))
                    pe.wait_ge(group_staged, n + 1)
                    pe.nop(nofuse=True)
                    for b in range(GH):
                        ins = pe.transpose(psG[0:D, slot(u), b * P:(b + 1) * P], x_staged[:, slot(u), b * D:(b + 1) * D], ident[:, :])
                    ins.then_inc(group_transposed, 1)

                def scores(p_, u):
                    n = L * NG + p_ * GP + u
                    pe.wait_ge(rT_ready, n + 1)
                    wait(pe, scores_kept, n + 1 - lag(u))
                    for b in range(GH):
                        ins = pe.matmul(psG[:, 4 + slot(u), 2 * b:2 * b + 2], rT[slot(u)][:, b * P:(b + 1) * P], att[L][:, :], start=True, stop=True)
                    ins.then_inc(scores_ready, 1)

                def node_piece(p_):
                    for u in range(GP):
                        if not (isinstance(p_, int) and p_ == PIECES - 1 and u == GP - 1):
                            transposes(p_, u + 1)
                        n = L * NG + p_ * GP + u
                        pe.wait_ge(hT_ready, n + 1)
                        wait(pe, rT_ready, n + 1 - lag(u))
                        pe.matmul(psG[:, 2 + slot(u), 0:GH * P], W[L][:, :], hT[slot(u)], start=True, stop=True).then_inc(hidden_multiplied, 1)
                        if not isinstance(p_, int) or p_ * GP + u > 0:
                            scores(p_, u - 1)
                pe.wait_ge(transposes_kept, 5 * RJ * 2)
                transposes(0, 0)
                steps(pe, 0, PIECES, node_piece)
                scores(PIECES - 1, GP - 1)

                pe.wait_ge(parts_ready, L + 1)

                def gather(i):
                    for t in range(2):
                        pe.wait_ge(one_hot_ready[t], base + i + 1)
                        wait(pe, selected[t], base + i)
                        for k in range(CH):
                            for m in range(3):
                                ins = pe.matmul(psG[:, 3 * t + k // 3, (k % 3) * HI:(k % 3 + 1) * HI],
                                                ones_lo[:, t, k * P:(k + 1) * P], ab_parts[:, m, t, :], start=m == 0, stop=m == 2)
                        ins.then_inc(gathered[t], 1)

                def col_parts(t, h, b_window, out_of, waited):
                    pe.wait_ge(one_hot_ready[1], base + t + 1)
                    wait(pe, selected[1], base + t + 1 - waited)
                    for k in range(CH):
                        ins = pe.matmul(out_of[:, 3 * k:3 * k + 3], window_one_hot[:, h, k * P:(k + 1) * P], b_window, start=True, stop=True)
                    ins.then_inc(gathered[1], 1)

                def gather_local(i):
                    for h in range(2):
                        t = i * 2 + h
                        pe.wait_ge(one_hot_ready[0], L * NA + t + 1)
                        wait(pe, selected[0], L * NA + t - 1)
                        for k in range(CH):
                            for m in range(3):
                                ins = pe.matmul(psG[:, 3 * h + k // 3, (k % 3) * HI:(k % 3 + 1) * HI],
                                                ones_lo[:, h, k * P:(k + 1) * P], ab_parts[:, m, 0, :], start=m == 0, stop=m == 2)
                        ins.then_inc(gathered[0], 1)
                        pe.wait_ge(near_b_loaded[h], (L * NA // 2 + i + 1) * 16)
                        col_parts(t, h, b_window[:, h, 0:3], psR[:, 0, :], 1)

                def gather_cols(i):
                    for u in range(FAR):
                        pe.wait_ge(far_b_loaded[u], (i - NA // FAR + L * NB // FAR + 1) * 16)
                        col_parts(i * FAR + u, u % 2, b_window[:, u, 0:3], psG[:, u % 2, :], 2)

                def scatter(i):
                    for h in range(2):
                        t = i * 2 + h
                        pe.wait_ge(hi_one_hot_ready, base + t + 1)
                        for k in range(CH):
                            if k < CH - 1:
                                pe.wait_ge(weighted_by_act, (base + t) * (CH - 1) + k + 1)
                            else:
                                pe.wait_ge(weighted_by_dve, base + t + 1)
                            ins = pe.matmul(psR[:, 1, 0:HI], lo_weighted[L][:, h, k, :], hi_one_hot[L][:, h, k, :], start=False, stop=False)
                        ins.then_inc(sums_added, 1)
                with pe.If(is_local):
                    steps(pe, 0, NA // 2, gather_local)
                with pe.Else():
                    steps(pe, 0, NS, gather)
                pe.matmul(psR[:, 1, 0:HI], zero[:, 0:P], zero[:, 0:HI], start=True, stop=False)
                steps(pe, 0, NA // 2, scatter)
                with pe.If(is_local):
                    pe.wait_ge(selected[0], NA * (L + 1))
                    steps(pe, NA // FAR, NS // FAR, gather_cols)
                with pe.Else():
                    pe.nop()
                steps(pe, NA // 2, NS // 2, scatter)
                pe.matmul(psR[:, 1, 0:HI], zero[:, 0:P], zero[:, 0:HI], start=False, stop=True).then_inc(row_sums_ready, 1)

                def body(i, by_window):
                    for h in range(2):
                        t = i * 2 + h
                        if by_window:
                            pe.wait_ge(window_one_hot_ready, base + t + 1)
                            pe.wait_ge(y_window_loaded[h], (base // 2 + i + 1) * 16)
                            wait(pe, y_kept, base + t - 1)
                            for k in range(CH):
                                ins = pe.matmul(psG[:, 2 + h, k * D:(k + 1) * D], window_one_hot_f32[:, h, k * P:(k + 1) * P], y_window[:, h, :], start=True, stop=True)
                            ins.then_inc(y_spread, 1)
                            pe.wait_ge(y_kept, base + t + 1)
                        else:
                            pe.wait_ge(y_fetched[h], (base // 2 + i + 1) * 16 * CH)
                        pe.wait_ge(merge_ready, base + t + 1)
                        wait(pe, message_ready, base + t - 1)
                        for k in range(CH):
                            ins = pe.matmul(psG[:, h, k * D:(k + 1) * D], merge[:, h, k, :], y_edge[:, h, k, :], start=True, stop=True)
                        ins.then_inc(merged, 1)
                with pe.If(is_local):
                    steps(pe, 0, NS // 2, lambda i: body(i, True))
                with pe.Else():
                    steps(pe, 0, NS // 2, lambda i: body(i, False))


_PARAMS = ['nbW', 'nbb', 'selfW', 'selfb', 'attW', 'attb']
_INS = ['x', 'src', 'dst', 'edge_weight1'] + [f'L0_gnn_{p}{L}' for L in range(2) for p in _PARAMS]


def kernel(**inputs):
    import numpy as _np
    import concourse.bacc as _bacc
    from concourse import mybir as _mybir
    from concourse.bass_utils import run_bass_kernel_spmd as _run
    nc = _bacc.Bacc("TRN2", target_bir_lowering=False, num_devices=1)
    arrays, args = {}, []
    for name in _INS:
        a = _np.ascontiguousarray(inputs[name])
        arrays[f"in_{name}_dram"] = a
        args.append(nc.dram_tensor(f"in_{name}_dram", a.shape, _mybir.dt.from_np(a.dtype), kind="ExternalInput").ap())
    out = nc.dram_tensor("out_0_dram", (N, D), _mybir.dt.float32, kind="ExternalOutput").ap()
    build(nc, *args[:4], [args[4:10], args[10:16]], out)
    r = _run(nc, [arrays], core_ids=[0])
    return r.results[0]["out_0_dram"]
```
